# Optimizing a Trainium2 kernel written in Bass

```python
import numpy as np
import jax
import jax.numpy as jnp

def _softmax(x, axis=-1):
    return jax.nn.softmax(x, axis=axis)

def _gelu(x):
    return jax.nn.gelu(x, approximate=True)

def _silu(x):
    return jax.nn.silu(x)

def _sigmoid(x):
    return jax.nn.sigmoid(x)

def _layernorm(x, axis=-1, eps=1e-05):
    m = jnp.mean(x, axis=axis, keepdims=True)
    v = jnp.var(x, axis=axis, keepdims=True)
    return (x - m) / jnp.sqrt(v + eps)

def _scatter_add(tgt, idx, src, axis=0):
    return tgt.at[idx].add(src)

def _segment_sum(src, seg, n):
    return jax.ops.segment_sum(src, seg, n)
kernel_name = 'mk_seq_postln_d1_jaxref_r4_944a29'

def setup_inputs(seed: int=0):
    np.random.seed(seed)
    _w = jnp.asarray

    def _L0_attn_setup():
        import jax, jax.numpy as jnp
        import numpy as np
        BATCH, SEQ, D_MODEL, N_HEADS, D_HEAD = (2, 512, 512, 16, 128)
        ATTN_SCALE = np.sqrt(D_HEAD).astype(np.float32)
        IGNORE = jnp.float32(-100000.0)
        key = jax.random.key(seed)
        ks = jax.random.split(key, 5)
        init = 1.0 / np.sqrt(D_MODEL)
        return {'x': jax.random.normal(ks[0], (BATCH, SEQ, D_MODEL), jnp.float32), 'W_Q': jax.random.normal(ks[1], (N_HEADS, D_MODEL, D_HEAD), jnp.float32) * init, 'W_K': jax.random.normal(ks[2], (N_HEADS, D_MODEL, D_HEAD), jnp.float32) * init, 'W_V': jax.random.normal(ks[3], (N_HEADS, D_MODEL, D_HEAD), jnp.float32) * init, 'W_O': jax.random.normal(ks[4], (N_HEADS, D_HEAD, D_MODEL), jnp.float32) * init, 'b_Q': jnp.zeros((N_HEADS, D_HEAD), jnp.float32), 'b_K': jnp.zeros((N_HEADS, D_HEAD), jnp.float32), 'b_V': jnp.zeros((N_HEADS, D_HEAD), jnp.float32), 'b_O': jnp.zeros((D_MODEL,), jnp.float32)}
    _L0_attn_in = _L0_attn_setup()

    def _L0_ffn_setup():
        import jax, jax.numpy as jnp
        import numpy as np
        D_MODEL = 512
        D_FF = 2048

        def absmean_quant(w):
            scale = jnp.mean(jnp.abs(w))
            mask = (jnp.abs(w) >= scale * 0.7).astype(w.dtype)
            return jnp.sign(w) * mask
        key = jax.random.key(seed)
        k_x, k_w1, k_w2 = jax.random.split(key, 3)
        x = jax.random.normal(k_x, (4, 1024, D_MODEL), dtype=jnp.float32)
        w1 = jax.random.normal(k_w1, (D_FF, D_MODEL), dtype=jnp.float32)
        b1 = jnp.zeros((D_FF,), dtype=jnp.float32)
        w2 = jax.random.normal(k_w2, (D_MODEL, D_FF), dtype=jnp.float32)
        b2 = jnp.zeros((D_MODEL,), dtype=jnp.float32)
        return {'x': x, 'w1': w1, 'b1': b1, 'w2': w2, 'b2': b2}
    _L0_ffn_in = _L0_ffn_setup()
    _d = {'L0_attn_x': _L0_attn_in['x'], 'L0_attn_W_Q': _L0_attn_in['W_Q'], 'L0_attn_W_K': _L0_attn_in['W_K'], 'L0_attn_W_V': _L0_attn_in['W_V'], 'L0_attn_W_O': _L0_attn_in['W_O'], 'L0_attn_b_Q': _L0_attn_in['b_Q'], 'L0_attn_b_K': _L0_attn_in['b_K'], 'L0_attn_b_V': _L0_attn_in['b_V'], 'L0_attn_b_O': _L0_attn_in['b_O'], 'L0_ffn_w1': _L0_ffn_in['w1'], 'L0_ffn_b1': _L0_ffn_in['b1'], 'L0_ffn_w2': _L0_ffn_in['w2'], 'L0_ffn_b2': _L0_ffn_in['b2']}
    _x0 = _d['L0_attn_x']
    _d['L0_attn_x'] = jax.random.normal(jax.random.fold_in(jax.random.key(seed), 1), (1, 2048, 512), dtype=_x0.dtype)
    del _x0
    return _d

def reference(L0_attn_x, L0_attn_W_Q, L0_attn_W_K, L0_attn_W_V, L0_attn_W_O, L0_attn_b_Q, L0_attn_b_K, L0_attn_b_V, L0_attn_b_O, L0_ffn_w1, L0_ffn_b1, L0_ffn_w2, L0_ffn_b2):

    def _L0_attn_ref(x, W_Q, W_K, W_V, W_O, b_Q, b_K, b_V, b_O):
        import jax, jax.numpy as jnp
        import numpy as np
        BATCH, SEQ, D_MODEL, N_HEADS, D_HEAD = (2, 512, 512, 16, 128)
        ATTN_SCALE = np.sqrt(D_HEAD).astype(np.float32)
        IGNORE = jnp.float32(-100000.0)
        q = jnp.einsum('bpd,hde->bphe', x, W_Q) + b_Q
        k = jnp.einsum('bpd,hde->bphe', x, W_K) + b_K
        v = jnp.einsum('bpd,hde->bphe', x, W_V) + b_V
        scores = jnp.einsum('bqhe,bkhe->bhqk', q, k) / ATTN_SCALE
        S = x.shape[1]
        causal = jnp.tril(jnp.ones((S, S), bool))
        scores = jnp.where(causal, scores, IGNORE)
        attn = jax.nn.softmax(scores, axis=-1)
        z = jnp.einsum('bkhe,bhqk->bqhe', v, attn)
        out = jnp.einsum('bqhe,hed->bqd', z, W_O) + b_O
        return out

    def _L0_ffn_ref(x, w1, b1, w2, b2):
        import jax, jax.numpy as jnp
        import numpy as np
        D_MODEL = 512
        D_FF = 2048

        def absmean_quant(w):
            scale = jnp.mean(jnp.abs(w))
            mask = (jnp.abs(w) >= scale * 0.7).astype(w.dtype)
            return jnp.sign(w) * mask
        w1_q = absmean_quant(w1)
        w2_q = absmean_quant(w2)
        h = jnp.einsum('bsd,fd->bsf', x, w1_q) + b1
        h = jax.nn.gelu(h, approximate=False)
        out = jnp.einsum('bsf,df->bsd', h, w2_q) + b2
        return out
    x = L0_attn_x
    x = _layernorm(x + _L0_attn_ref(x, L0_attn_W_Q, L0_attn_W_K, L0_attn_W_V, L0_attn_W_O, L0_attn_b_Q, L0_attn_b_K, L0_attn_b_V, L0_attn_b_O), axis=-1)
    x = _layernorm(x + _L0_ffn_ref(x, L0_ffn_w1, L0_ffn_b1, L0_ffn_w2, L0_ffn_b2), axis=-1)
    return x

_drawn_inputs = setup_inputs


def setup_inputs(seed=0):
    import zlib

    import numpy as np

    out = dict(_drawn_inputs(seed))
    spreads = {'L0_attn_b_Q': (0.0, 0.552),
     'L0_attn_b_K': (0.0, 0.8),
     'L0_attn_b_V': (0.0, 0.1),
     'L0_attn_b_O': (0.0, 0.1),
     'L0_ffn_b1': (0.0, 0.8),
     'L0_ffn_b2': (0.0, 0.8)}
    factors = {}
    for name, (base, spread) in spreads.items():
        noise = np.random.default_rng([zlib.crc32(name.encode()), seed]).standard_normal(out[name].shape)
        drawn = base * np.exp(spread * noise) if base else spread * noise
        out[name] = jnp.asarray(drawn.astype(out[name].dtype))
    for name, factor in factors.items():
        out[name] = (out[name] * factor).astype(out[name].dtype)
    return out
```

```python
from contextlib import ExitStack

import concourse.bass as bass
from concourse import mybir

F32 = mybir.dt.float32
F32R = mybir.dt.float32r
BF16 = mybir.dt.bfloat16
ALU = mybir.AluOpType
ACT = mybir.ActivationFunctionType
AX_X = mybir.AxisListType.X

P = 128
BANK = 512
EPS = 1e-5
MASKED = -1.0e5

GROUPS = 4
RING = 3
SRING = 4
PTRING = 4
UNITS = 60
KTS = 40
EVENTS = 40
CARRY_U = 17
CARRY_K = 16


def event(g, j, b):
    return sum(4 * (n + 1) for n in range(g)) + j * (g + 1) + b


def head_order(first):
    items, u, m = [], 0, 0
    for g in range(GROUPS):
        gp = (g - 1) % GROUPS
        carried = -EVENTS if g == 0 else 0
        prev = not (first and g == 0)
        tail = [("exp", gp, 3, b, event(gp, 3, b) + carried) for b in range(gp + 1)] if prev else []
        items += tail[:2]
        items.append(("q", g, u)); u += 1
        items += tail[2:3]
        items.append(("k", g, u)); u += 1
        items += tail[3:]
        items.append(("vt", g, u)); u += 1
        m0 = m
        pend = []
        for j in range(GROUPS):
            kts = [j * (gp + 1) + n for n in range(gp + 1)] if prev else []
            for b in range(g + 1):
                lead = 2 if b == 0 else 1
                while kts and lead:
                    kt = kts.pop(0)
                    items.append(("kt", gp, kt, u, m, carried)); pend.append((kt, u, m)); u += 1; m += 1
                    lead -= 1
                    if len(pend) > 2:
                        items.append(("pv", gp) + pend.pop(0))
                if j:
                    items.append(("exp", g, j - 1, b, event(g, j - 1, b)))
                items.append(("s", g, j, b, event(g, j, b)))
            for kt in kts:
                items.append(("kt", gp, kt, u, m, carried)); pend.append((kt, u, m)); u += 1; m += 1
                if len(pend) > 2:
                    items.append(("pv", gp) + pend.pop(0))
            if j == 0 and prev:
                items.append(("sum", gp, carried))
        items.append(("v", g, u)); u += 1
        items += [("pv", gp) + x for x in pend]
        if prev:
            items.append(("norm", gp, u, g)); u += 1
    return items


def tail_order():
    gp, items, pend = GROUPS - 1, [], []
    items += [("exp", gp, 3, b, event(gp, 3, b) - EVENTS) for b in range(gp + 1)]
    items.append(("sum", gp, -EVENTS))
    for kt in range(4 * (gp + 1)):
        items.append(("kt", gp, kt, kt, kt, -EVENTS)); pend.append((kt, kt, kt))
        if len(pend) > 2:
            items.append(("pv", gp) + pend.pop(0))
    items += [("pv", gp) + x for x in pend]
    items.append(("norm", gp, 4 * (gp + 1), 0))
    return items


def attention_block(nc, H, T, DM, DH, xT, wq, wk, wv, bqkv, f1, f2, abs_sums, z_dram):
    C = DM // P
    SCALE = float(DH) ** -0.5
    NEG = MASKED / SCALE
    assert DH == P and T == GROUPS * BANK and C == 4
    with ExitStack() as ctx:
        def sb(name, shape, dt=F32):
            return ctx.enter_context(nc.sbuf_tensor(name, shape, dt))

        def sem(name):
            return ctx.enter_context(nc.semaphore(name))

        x_hi = sb("x_hi", [P, C, T], F32R)
        x_lo = sb("x_lo", [P, C, T], F32R)
        k_hi = sb("k_hi", [P, T], F32R)
        k_lo = sb("k_lo", [P, T], F32R)
        v_hi = sb("v_hi", [P, T], F32R)
        v_lo = sb("v_lo", [P, T], F32R)
        q_hi = sb("q_hi", [P, BANK], F32R)
        q_lo = sb("q_lo", [P, BANK], F32R)
        vt = sb("vt", [P, BANK])
        probs_even = sb("probs_even", [P, GROUPS, 3 * BANK])
        probs_odd = sb("probs_odd", [P, GROUPS, 4 * BANK])
        pt_hi = sb("pt_hi", [P, PTRING, BANK], F32R)
        pt_lo = sb("pt_lo", [P, PTRING, BANK], F32R)
        z_raw = sb("z_raw", [P, BANK])
        z_out = sb("z_out", [P, 2, BANK])
        w_raw = sb("w_raw", [P, 3, C, DH])
        w_hi = sb("w_hi", [P, 3, C, DH], F32R)
        w_lo = sb("w_lo", [P, 3, C, DH], F32R)
        b_raw = sb("b_raw", [P, 4])
        b_cur = sb("b_cur", [P, 4])
        zeros = sb("zeros", [P, 4])
        ident = sb("ident", [P, P])
        ident_bf = sb("ident_bf", [P, P], BF16)
        mask_bf = sb("mask_bf", [P, P], BF16)
        f_raw = sb("f_raw", [P, 2, DM])
        mx = sb("mx", [P, 2, GROUPS])
        mx_scaled = sb("mx_scaled", [P, GROUPS])
        neg_max = sb("neg_max", [P, 2, GROUPS])
        sums = sb("sums", [P, 2, GROUPS, GROUPS])
        total = sb("total", [P, GROUPS])
        rinv = sb("rinv", [P, GROUPS])
        probs = [probs_even, probs_odd]

        score = [ctx.enter_context(nc.psum_tensor(f"score{n}", [P, BANK], F32)) for n in range(SRING)]
        ring = [ctx.enter_context(nc.psum_tensor(f"ring{n}", [P, BANK], F32)) for n in range(RING)]
        z_ps = ctx.enter_context(nc.psum_tensor("z_ps", [P, BANK], F32))

        x_loaded = [sem(f"x_loaded{g}") for g in range(GROUPS)]
        x_hi_ready = sem("x_hi_ready")
        x_lo_ready = sem("x_lo_ready")
        w_loaded = sem("w_loaded")
        w_part = sem("w_part")
        w_ready = sem("w_ready")
        consts = sem("consts")
        ring_full = sem("ring_full")
        ring_hi = sem("ring_hi")
        ring_lo = sem("ring_lo")
        score_full = sem("score_full")
        max_part = sem("max_part")
        max_ready = sem("max_ready")
        exp_done = sem("exp_done")
        sum_part = sem("sum_part")
        rinv_ready = sem("rinv_ready")
        z_stored = [sem(f"z_stored{n}") for n in range(2)]
        f_loaded = sem("f_loaded")
        f_summed = sem("f_summed")

        def count(eng, s, per_head, h, n):
            if isinstance(h, int):
                if h * per_head + n > 0:
                    eng.wait_ge(s, h * per_head + n)
            else:
                assert per_head + n > 0
                eng.wait_ge(s, h * per_head + n)

        def bank(first, u):
            return (u if first else u - CARRY_U) % RING

        def slot(first, m):
            return (m if first else m - CARRY_K) % PTRING

        def for_heads(eng, run):
            run(0, head_order(True), True)
            with eng.Fori(1, H) as h:
                run(h, head_order(False), False)
            run(H, tail_order(), False)

        LAST_VT = [it[2] for it in head_order(False) if it[0] == "vt"][-1] - CARRY_U

        with nc.Block() as block:

            @block.sync
            def _(sp):
                for g in range(GROUPS):
                    blk = slice(g * BANK, (g + 1) * BANK)
                    sp.dma_start(probs_odd[:, :, blk], xT.rearrange("(c p) t -> p c t", p=P)[:, :, blk]
                                 ).then_inc(x_loaded[g], 16)

                f1_v, f2_v = (f.rearrange("(n p) d -> n p d", p=P) for f in (f1, f2))

                def load_ffn_slices(h):
                    for n, f in enumerate((f1_v, f2_v)):
                        count(sp, f_summed, 2, h, 0)
                        sp.dma_start(f_raw[:, n, :], f[h, :, :]).then_inc(f_loaded, 16)

                def run(h, order, first):
                    if order[-1][0] == "norm" and order[-1][1] == GROUPS - 2:
                        load_ffn_slices(h)
                    for it in order:
                        if it[0] == "norm":
                            _, gp, u, n = it
                            hz = h - 1 if gp == GROUPS - 1 else h
                            count(sp, ring_lo, UNITS, h, u + 1 - (0 if first else CARRY_U))
                            slot_z = gp % 2
                            sp.dma_start(z_dram[gp, :, :, hz, :].rearrange("i e q -> e i q"),
                                         z_out[:, slot_z, :].rearrange("e (i q) -> e i q", q=P)
                                         ).then_inc(z_stored[slot_z], 16)

                for_heads(sp, run)
                for s in z_stored:
                    sp.wait_ge(s, 16 * GROUPS * H // 2)

            @block.gpsimd
            def _(pool):
                pool.memset(ident[:], 0.0).then_inc(consts, 1)
                pool.memset(ident_bf[:], 0.0).then_inc(consts, 1)
                pool.memset(mask_bf[:], 0.0).then_inc(consts, 1)
                pool.memset(zeros[:], 0.0).then_inc(consts, 1)
                pool.wait_ge(consts, 4)
                for m in (ident, ident_bf):
                    pool.affine_select(out=m[:], in_=m[:], compare_op=ALU.not_equal, fill=1.0, base=0,
                                       pattern=[[-1, P]], channel_multiplier=1).then_inc(consts, 1)
                pool.affine_select(out=mask_bf[:], in_=mask_bf[:], compare_op=ALU.is_ge, fill=NEG, base=0,
                                   pattern=[[-1, P]], channel_multiplier=1).then_inc(consts, 1)

                def load(h):
                    for n, w in enumerate((wq, wk, wv)):
                        pool.dma_start(w_raw[:, n, :, :], w[h, :, :].rearrange("(c p) e -> p c e", p=P)
                                       ).then_inc(w_loaded, 16)
                    pool.dma_start(b_raw[:, 0:3], bqkv[h, :, :]).then_inc(w_loaded, 16)

                def split(h):
                    pool.wait_ge(w_loaded, h * 64 + 64)
                    pool.tensor_tensor(b_cur[:, 0:3], b_raw[:, 0:3], zeros[:, 0:3], ALU.add).then_inc(w_part, 1)
                    for n in range(3):
                        pool.tensor_scalar(w_hi[:, n, :, :], w_raw[:, n, :, :], 1.0, 0.0, ALU.mult, ALU.add
                                           ).then_inc(w_part, 1)
                    for n in range(3):
                        pool.wait_ge(w_part, h * 6 + (n + 2))
                        last = pool.tensor_tensor(w_lo[:, n, :, :], w_raw[:, n, :, :],
                                                  w_hi[:, n, :, :].bitcast(F32), ALU.subtract)
                        last.then_inc(w_part if n < 2 else w_ready, 1)

                load(0)
                split(0)
                with pool.Fori(1, H) as h:
                    pool.wait_ge(w_part, h * 6)
                    pool.wait_ge(w_ready, h)
                    load(h)
                    pool.wait_ge(ring_lo, (h - 1) * UNITS + (LAST_VT + 1))
                    split(h)

            @block.scalar
            def _(act):
                def hi_part(out, src, bias=None):
                    if bias is None:
                        return nc.scalar.activation(out, src, ACT.Copy)
                    return nc.scalar.activation(out, src, ACT.Identity, bias=bias)

                for g in range(GROUPS):
                    blk = slice(g * BANK, (g + 1) * BANK)
                    act.wait_ge(x_loaded[g], 16)
                    hi_part(x_hi[:, :, blk], probs_odd[:, :, blk]).then_inc(x_hi_ready, 1)

                def run(h, order, first):
                    off = 0 if first else CARRY_U
                    for it in order:
                        kind, g = it[0], it[1]
                        if kind in ("q", "k", "vt", "v"):
                            u = it[2]
                            src = ring[bank(first, u)]
                            count(act, ring_full, UNITS, h, u + 1 - off)
                            if kind == "q":
                                i = hi_part(q_hi[:], src[:], b_cur[:, 0:1])
                            elif kind == "k":
                                i = hi_part(k_hi[:, g * BANK:(g + 1) * BANK], src[:], b_cur[:, 1:2])
                            elif kind == "vt":
                                i = hi_part(vt[:, 0:BANK // 2], src[:, 0:BANK // 2], b_cur[:, 2:3])
                            else:
                                i = hi_part(v_hi[:, g * BANK:(g + 1) * BANK], src[:])
                            i.then_inc(ring_hi, 1)
                        elif kind == "kt":
                            _, _, kt, u, m, _ = it
                            c0 = max(0, kt - 4 * g) * P
                            count(act, ring_full, UNITS, h, u + 1 - off)
                            hi_part(pt_hi[:, slot(first, m), c0:], ring[bank(first, u)][:, c0:]
                                    ).then_inc(ring_hi, 1)
                        elif kind == "norm":
                            u = it[2]
                            count(act, ring_full, UNITS, h, u + 1 - off)
                            hi_part(z_raw[:], z_ps[:]).then_inc(ring_hi, 1)
                        elif kind == "exp":
                            _, _, j, b, e = it
                            w = P * (j + 1) if b == g else BANK
                            hh = 4 * g + j + 1 - (16 if e < 0 else 0)
                            count(act, max_ready, 4 * GROUPS, h, hh)
                            nc.scalar.activation(probs[g % 2][:, j, b * BANK:b * BANK + w],
                                                 score[e % SRING][:, 0:w], ACT.Exp,
                                                 bias=neg_max[:, g % 2, j:j + 1], scale=SCALE,
                                                 accum_out=sums[:, g % 2, j, b:b + 1]).then_inc(exp_done, 1)

                for_heads(act, run)

            @block.vector
            def _(dve):
                for g in range(GROUPS):
                    blk = slice(g * BANK, (g + 1) * BANK)
                    dve.wait_ge(x_hi_ready, g + 1)
                    dve.tensor_tensor(x_lo[:, :, blk], probs_odd[:, :, blk], x_hi[:, :, blk].bitcast(F32),
                                      ALU.subtract).then_inc(x_lo_ready, 1)

                def run(h, order, first):
                    off = 0 if first else CARRY_U
                    for it in order:
                        kind, g = it[0], it[1]
                        if kind in ("q", "k", "vt", "v"):
                            u = it[2]
                            src = ring[bank(first, u)]
                            blk = slice(g * BANK, (g + 1) * BANK)
                            count(dve, ring_hi, UNITS, h, u + 1 - off)
                            if kind == "q":
                                i = dve.scalar_tensor_tensor(out=q_lo[:], in0=src[:], scalar=b_cur[:, 0:1],
                                                             in1=q_hi[:].bitcast(F32), op0=ALU.add,
                                                             op1=ALU.subtract)
                            elif kind == "k":
                                i = dve.scalar_tensor_tensor(out=k_lo[:, blk], in0=src[:], scalar=b_cur[:, 1:2],
                                                             in1=k_hi[:, blk].bitcast(F32), op0=ALU.add,
                                                             op1=ALU.subtract)
                            elif kind == "vt":
                                i = dve.tensor_scalar(vt[:, BANK // 2:], src[:, BANK // 2:], b_cur[:, 2:3], None,
                                                      ALU.add)
                            else:
                                i = dve.tensor_tensor(v_lo[:, blk], src[:], v_hi[:, blk].bitcast(F32),
                                                      ALU.subtract)
                            i.then_inc(ring_lo, 1)
                        elif kind == "kt":
                            _, _, kt, u, m, _ = it
                            c0 = max(0, kt - 4 * g) * P
                            s = slot(first, m)
                            count(dve, ring_hi, UNITS, h, u + 1 - off)
                            dve.tensor_tensor(pt_lo[:, s, c0:], ring[bank(first, u)][:, c0:],
                                              pt_hi[:, s, c0:].bitcast(F32), ALU.subtract).then_inc(ring_lo, 1)
                        elif kind == "norm":
                            _, gp, u, n = it
                            stores = gp // 2 - (2 if gp == GROUPS - 1 else 0)
                            count(dve, z_stored[gp % 2], 16 * 2, h, 16 * stores)
                            count(dve, ring_hi, UNITS, h, u + 1 - off)
                            dve.tensor_tensor(z_out[:, gp % 2, :], ring[bank(first, u)][:], z_raw[:],
                                              ALU.mult).then_inc(ring_lo, 1)
                        elif kind == "s":
                            _, _, j, b, e = it
                            w = P * (j + 1) if b == g else BANK
                            count(dve, score_full, EVENTS, h, e + 1)
                            dve.tensor_reduce(mx[:, j % 2, b:b + 1], score[e % SRING][:, 0:w], AX_X, ALU.max
                                              ).then_inc(max_part, 1)
                            if b == g:
                                count(dve, max_part, EVENTS, h, e + 1)
                                dve.tensor_scalar(mx_scaled[:, 0:g + 1], mx[:, j % 2, 0:g + 1], -SCALE, None,
                                                  ALU.mult, ALU.min, accum_out=neg_max[:, g % 2, j:j + 1]
                                                  ).then_inc(max_ready, 1)
                        elif kind == "sum":
                            _, _, carried = it
                            n_sum = g + 1 - (GROUPS if carried else 0)
                            count(dve, exp_done, EVENTS, h, event(g, 3, g) + 1 + carried)
                            dve.tensor_reduce(total[:], sums[:, g % 2, :, 0:g + 1], AX_X, ALU.add
                                              ).then_inc(sum_part, 1)
                            count(dve, sum_part, GROUPS, h, n_sum)
                            dve.reciprocal(rinv[:], total[:]).then_inc(rinv_ready, 1)
                            if g == 0:
                                dve.wait_ge(f_loaded, h * 32 + 32)
                                for n in range(2):
                                    column = abs_sums[:, n, bass.ds(h, 1)] if not isinstance(h, int) \
                                        else abs_sums[:, n, h:h + 1]
                                    dve.tensor_reduce(column, f_raw[:, n, :], AX_X, ALU.add,
                                                      apply_absolute_value=True).then_inc(f_summed, 1)

                for_heads(dve, run)

            @block.tensor
            def _(pe):
                pe.wait_ge(consts, 7)

                def project(out, n, g):
                    blk = slice(g * BANK, (g + 1) * BANK)
                    for c in range(C):
                        nc.tensor.matmul(out, w_hi[:, n, c, :], x_hi[:, c, blk], start=(c == 0), stop=False)
                        nc.tensor.matmul(out, w_hi[:, n, c, :], x_lo[:, c, blk], start=False, stop=False)
                        last = nc.tensor.matmul(out, w_lo[:, n, c, :], x_hi[:, c, blk], start=False,
                                                stop=(c == C - 1))
                    return last

                def run(h, order, first):
                    off = 0 if first else CARRY_U
                    for it in order:
                        kind, g = it[0], it[1]
                        if kind in ("q", "k", "vt", "v"):
                            u = it[2]
                            out = ring[bank(first, u)]
                            if kind == "q" and g == 0:
                                pe.wait_ge(w_ready, h + 1)
                            if kind == "q" and first:
                                pe.wait_ge(x_lo_ready, g + 1)
                            count(pe, ring_lo, UNITS, h, u - RING + 1 - off)
                            if kind == "v":
                                u_vt = [x[2] for x in order if x[0] == "vt" and x[1] == g][0]
                                count(pe, ring_lo, UNITS, h, u_vt + 1 - off)
                                for t in range(GROUPS):
                                    last = nc.tensor.transpose(out[:, t * P:(t + 1) * P],
                                                               vt[:, t * P:(t + 1) * P], ident[:])
                            else:
                                last = project(out[:], ("q", "k", "vt").index(kind), g)
                            last.then_inc(ring_full, 1)
                        elif kind == "kt":
                            _, _, kt, u, m, carried = it
                            count(pe, ring_lo, UNITS, h, u - RING + 1 - off)
                            count(pe, exp_done, EVENTS, h, event(g, 3, kt // 4) + 1 + carried)
                            for j in range(max(0, kt - 4 * g), GROUPS):
                                last = nc.tensor.transpose(ring[bank(first, u)][:, j * P:(j + 1) * P],
                                                           probs[g % 2][:, j, kt * P:(kt + 1) * P], ident[:])
                            last.then_inc(ring_full, 1)
                        elif kind == "pv":
                            _, _, kt, u, m = it
                            c0 = max(0, kt - 4 * g) * P
                            s = slot(first, m)
                            vs = slice(kt * P, (kt + 1) * P)
                            end = kt == 4 * g + 3
                            count(pe, ring_lo, UNITS, h, u + 1 - off)
                            nc.tensor.matmul(z_ps[:, c0:], v_hi[:, vs], pt_hi[:, s, c0:], start=(kt == 0), stop=False)
                            nc.tensor.matmul(z_ps[:, c0:], v_hi[:, vs], pt_lo[:, s, c0:], start=False, stop=False)
                            nc.tensor.matmul(z_ps[:, c0:], v_lo[:, vs], pt_hi[:, s, c0:], start=False, stop=end)
                        elif kind == "norm":
                            _, gp, u, n = it
                            count(pe, ring_lo, UNITS, h, u - RING + 1 - off)
                            count(pe, rinv_ready, GROUPS, h, gp + 1 - (GROUPS if gp == GROUPS - 1 else 0))
                            for j in range(GROUPS):
                                last = nc.tensor.transpose(ring[bank(first, u)][:, j * P:(j + 1) * P],
                                                           rinv[:, j:j + 1].to_broadcast([P, P]), ident[:])
                            last.then_inc(ring_full, 1)
                        elif kind == "s":
                            _, _, j, b, e = it
                            w = P * (j + 1) if b == g else BANK
                            keys = slice(b * BANK, b * BANK + w)
                            out = score[e % SRING][:, 0:w]
                            qs = slice(j * P, (j + 1) * P)
                            if j == 0 and b == 0:
                                u = [x[2] for x in order if x[0] == "k" and x[1] == g][0]
                                count(pe, ring_lo, UNITS, h, u + 1 - off)
                            count(pe, exp_done, EVENTS, h, e - SRING + 1)
                            nc.tensor.matmul(out, q_hi[:, qs], k_hi[:, keys], start=True, stop=False)
                            nc.tensor.matmul(out, q_hi[:, qs], k_lo[:, keys], start=False, stop=False)
                            last = nc.tensor.matmul(out, q_lo[:, qs], k_hi[:, keys], start=False, stop=(b < g))
                            if b == g:
                                last = nc.tensor.matmul(out[:, w - P:w], ident_bf[:], mask_bf[:], start=False,
                                                        stop=True)
                            last.then_inc(score_full, 1)

                for_heads(pe, run)



def post_norm(nc, dve, mv, var, r0, t1, t2, rstd, n, chain, base, var_ready, root, root_ready, turn):
    dve.tensor_scalar(var, mv[:, :, 1], EPS, None, ALU.add).then_inc(var_ready, 1)
    dve.wait_ge(root_ready, turn + 1)
    dve.reciprocal(r0, root).then_inc(chain, 1)
    dve.wait_ge(chain, base + 1)
    dve.tensor_tensor(t1, r0, r0, ALU.mult).then_inc(chain, 1)
    dve.wait_ge(chain, base + 2)
    dve.tensor_tensor(t2, t1, var, ALU.mult).then_inc(chain, 1)
    dve.wait_ge(chain, base + 3)
    dve.tensor_scalar(t1, t2, -0.5, 1.5, ALU.mult, ALU.add).then_inc(chain, 1)
    dve.wait_ge(chain, base + 4)
    dve.tensor_tensor(rstd, t1, r0, ALU.mult).then_inc(chain, 1)
    dve.wait_ge(chain, base + 5)


def projection_block(nc, H, T, DM, F, x, wo, bo, w1T, w2T, abs_sums, w1_t, w2_t, z_dram, x1_dram):
    TILES = T // P
    PAIRS = TILES // 2
    HALF = F * (DM // P) // PAIRS
    WO_PARTS = 8
    HP = H // WO_PARTS
    with ExitStack() as ctx:
        def sb(name, shape, dt=F32):
            return ctx.enter_context(nc.sbuf_tensor(name, shape, dt))

        def sem(name):
            return ctx.enter_context(nc.semaphore(name))

        wo_hi = sb("wo_hi", [P, H, DM], F32R)
        wo_lo = sb("wo_lo", [P, H, DM], F32R)
        wo_raw = sb("wo_raw", [P, 2, HP, DM])
        zt_raw = sb("zt_raw", [P, H, P])
        zt_hi = sb("zt_hi", [P, 2, H, P], F32R)
        zt_lo = sb("zt_lo", [P, 2, H, P], F32R)
        x_t = sb("x_t", [P, 2, DM])
        xb_t = sb("xb_t", [P, 2, DM])
        bo_all = sb("bo_all", [P, DM])
        r_t = sb("r_t", [P, DM])
        x1_t = sb("x1_t", [P, 2, DM])
        f_raw = sb("f_raw2", [P, HALF])
        below = sb("below", [P, HALF], BF16)
        ones = sb("ones", [P, P])
        sums = sb("sums2", [P, 2])
        thr = sb("thr", [P, 2])
        neg_thr = sb("neg_thr", [P, 2])
        st = sb("st", [P, nc.vector.BN_STATS_DIM])
        mv = sb("mv", [P, 1, nc.vector.BN_AGGR_DIM])
        small = sb("small", [P, 8])
        var, root, r0, t1, t2, rstd = (small[:, n:n + 1] for n in range(6))
        out_ps = [ctx.enter_context(nc.psum_tensor(f"out_ps{n}", [P, DM], F32)) for n in range(2)]
        sum_ps = ctx.enter_context(nc.psum_tensor("sum_ps", [P, 2], F32))

        wo_loaded = [sem(f"wo_loaded{n}") for n in range(2)]
        wo_hi_ready = sem("wo_hi_ready")
        wo_lo_ready = sem("wo_lo_ready")
        z_loaded = sem("z_loaded")
        z_hi_ready = sem("z_hi_ready")
        z_lo_ready = sem("z_lo_ready")
        x_loaded = [sem(f"x_loaded_s{n}") for n in range(2)]
        bo_loaded = sem("bo_loaded")
        xb_ready = sem("xb_ready")
        out_full = sem("out_full")
        r_ready = sem("r_ready")
        ln_step = sem("ln_step")
        ln_chain = sem("ln_chain")
        var_ready = sem("var_ready")
        root_ready = sem("root_ready")
        x1_ready = sem("x1_ready")
        x1_stored = [sem(f"x1_stored{n}") for n in range(2)]
        f_loaded = sem("f_loaded2")
        below_ready = sem("below_ready")
        ternary = sem("ternary")
        ones_ready = sem("ones_ready")
        sums_ready = sem("sums_ready")
        total_ready = sem("total_ready")
        scale_ready = sem("scale_ready")
        thr_ready = sem("thr_ready")

        x_v = x.rearrange("(i p) d -> i p d", p=P)
        x1_v = x1_dram.rearrange("(i p) d -> i p d", p=P)
        wo_v = wo.rearrange("h e d -> e h d")
        w2_v = w2T.rearrange("(n a p) d -> n p a d", p=P, a=HALF // DM)
        w1_flat = w1_t[:].rearrange("p c f -> p (c f)")
        w2_flat = w2_t[:].rearrange("p c d -> p (c d)")

        def after(eng, s, value, least):
            if least > 0:
                eng.wait_ge(s, value)

        def for_pairs(eng, pair):
            pair(0, 0)
            with eng.Fori(1, PAIRS - 1) as it:
                pair(it, 1)
            pair(PAIRS - 1, PAIRS - 1)

        with nc.Block() as block:

            @block.sync
            def _(sp):
                def load_z(i, least):
                    after(sp, z_lo_ready, i, least)
                    sp.dma_start(zt_raw[:], z_flat[i, :, :, :]).then_inc(z_loaded, 16)

                z_flat = z_dram.rearrange("g i e h q -> (g i) e h q")
                sp.dma_start(bo_all[:], bo.rearrange("(a d) -> a d", a=1).to_broadcast([P, DM])
                             ).then_inc(bo_loaded, 16)
                load_z(0, 0)
                for n in range(WO_PARTS):
                    if n >= 2:
                        sp.wait_ge(wo_lo_ready, n - 1)
                    sp.dma_start(wo_raw[:, n % 2, :, :], wo_v[:, n * HP:(n + 1) * HP, :]).then_inc(wo_loaded[n % 2], 16)

                def pair(it, least):
                    for p in range(2):
                        i = it * 2 + p
                        if not (isinstance(it, int) and i == TILES - 1):
                            load_z(i + 1, 2 * least + p + 1)
                        after(sp, xb_ready, i - 1, 2 * least + p - 1)
                        sp.dma_start(x_t[:, p, :], x_v[i, :, :]).then_inc(x_loaded[p], 16)
                        after(sp, ternary, i, 2 * least + p)
                        if p == 0:
                            sp.dma_start(f_raw[:], w1T[it, :, :]).then_inc(f_loaded, 16)
                        else:
                            sp.dma_start(f_raw[:].rearrange("p (a d) -> p a d", d=DM), w2_v[it, :, :, :]
                                         ).then_inc(f_loaded, 16)

                for_pairs(sp, pair)
                for s in x1_stored:
                    sp.wait_ge(s, 16 * PAIRS)

            @block.gpsimd
            def _(pool):
                pool.wait_ge(bo_loaded, 16)

                def pair(it, least):
                    for p in range(2):
                        i = it * 2 + p
                        pool.wait_ge(x_loaded[p], it * 16 + 16)
                        after(pool, r_ready, i - 1, 2 * least + p - 1)
                        pool.tensor_tensor(xb_t[:, p, :], x_t[:, p, :], bo_all[:], ALU.add).then_inc(xb_ready, 1)

                for_pairs(pool, pair)

            @block.scalar
            def _(act):
                def z_part(i, p):
                    act.wait_ge(z_loaded, i * 16 + 16)
                    nc.scalar.activation(zt_hi[:, p, :, :], zt_raw[:], ACT.Copy).then_inc(z_hi_ready, 1)

                z_part(0, 0)
                for n in range(WO_PARTS):
                    act.wait_ge(wo_loaded[n % 2], 16 * (n // 2 + 1))
                    nc.scalar.activation(wo_hi[:, n * HP:(n + 1) * HP, :], wo_raw[:, n % 2, :, :], ACT.Copy
                                         ).then_inc(wo_hi_ready, 1)

                def pair(it, least):
                    for p in range(2):
                        i = it * 2 + p
                        if not (isinstance(it, int) and i == TILES - 1):
                            after(act, out_full, i, 2 * least + p)
                            z_part(i + 1, 1 - p)
                        act.wait_ge(var_ready, i + 1)
                        nc.scalar.activation(root, var, ACT.Sqrt).then_inc(root_ready, 1)
                        act.wait_ge(x1_ready, i + 1)
                        act.dma_start(x1_v[i, :, :], x1_t[:, p, :]).then_inc(x1_stored[p], 16)

                for_pairs(act, pair)

            @block.vector
            def _(dve):
                def z_part(i, p):
                    dve.wait_ge(z_hi_ready, i + 1)
                    dve.tensor_tensor(zt_lo[:, p, :, :], zt_raw[:], zt_hi[:, p, :, :].bitcast(F32), ALU.subtract
                                      ).then_inc(z_lo_ready, 1)

                dve.memset(ones[:], 1.0).then_inc(ones_ready, 1)
                dve.tensor_reduce(sums[:], abs_sums[:], AX_X, ALU.add).then_inc(sums_ready, 1)
                z_part(0, 0)
                for n in range(WO_PARTS):
                    dve.wait_ge(wo_hi_ready, n + 1)
                    dve.tensor_tensor(wo_lo[:, n * HP:(n + 1) * HP, :], wo_raw[:, n % 2, :, :],
                                      wo_hi[:, n * HP:(n + 1) * HP, :].bitcast(F32), ALU.subtract
                                      ).then_inc(wo_lo_ready, 1)
                dve.wait_ge(total_ready, 1)
                dve.tensor_scalar(thr[:], sum_ps[:], 1.0 / (F * DM), 0.7, ALU.mult, ALU.mult).then_inc(scale_ready, 1)
                dve.wait_ge(scale_ready, 1)
                dve.tensor_scalar(neg_thr[:], thr[:], -1.0, None, ALU.mult).then_inc(thr_ready, 1)
                dve.wait_ge(thr_ready, 1)

                def pair(it, least):
                    for p in range(2):
                        i = it * 2 + p
                        if not (isinstance(it, int) and i == TILES - 1):
                            z_part(i + 1, 1 - p)
                        dve.wait_ge(out_full, i + 1)
                        dve.wait_ge(xb_ready, i + 1)
                        after(dve, x1_ready, i, 2 * least + p)
                        dve.tensor_tensor(r_t[:], out_ps[p][:], xb_t[:, p, :], ALU.add).then_inc(r_ready, 1)
                        dve.wait_ge(r_ready, i + 1)
                        dve.bn_stats(st[:], r_t[:]).then_inc(ln_step, 1)
                        dve.wait_ge(f_loaded, i * 16 + 16)
                        dve.tensor_scalar(below[:], f_raw[:], neg_thr[:, p:p + 1], None, ALU.is_le
                                          ).then_inc(below_ready, 1)
                        dve.wait_ge(ln_step, i * 2 + 1)
                        dve.wait_ge(below_ready, i + 1)
                        flat = (w1_flat, w2_flat)[p]
                        dve.scalar_tensor_tensor(out=flat[:, bass.ds(it * HALF, HALF)], in0=f_raw[:],
                                                 scalar=thr[:, p:p + 1], in1=below[:], op0=ALU.is_ge,
                                                 op1=ALU.subtract).then_inc(ternary, 1)
                        dve.bn_aggr(mv[:, 0, :], st[:]).then_inc(ln_step, 1)
                        dve.wait_ge(ln_step, i * 2 + 2)
                        post_norm(nc, dve, mv, var, r0, t1, t2, rstd, 1, ln_chain, i * 5, var_ready, root,
                                  root_ready, i)
                        after(dve, x1_stored[p], it * 16, least)
                        dve.tensor_scalar(x1_t[:, p, :], r_t[:], mv[:, 0, 0:1], rstd, ALU.subtract, ALU.mult
                                          ).then_inc(x1_ready, 1)

                for_pairs(dve, pair)

            @block.tensor
            def _(pe):
                pe.wait_ge(ones_ready, 1)
                pe.wait_ge(sums_ready, 1)
                nc.tensor.matmul(sum_ps[:], ones[:], sums[:], start=True, stop=True).then_inc(total_ready, 1)

                def pair(it, least):
                    for p in range(2):
                        i = it * 2 + p
                        pe.wait_ge(z_lo_ready, i + 1)
                        after(pe, r_ready, i - 1, 2 * least + p - 1)
                        for h in range(H):
                            if isinstance(it, int) and i == 0 and h % HP == 0:
                                pe.wait_ge(wo_lo_ready, h // HP + 1)
                            a_hi, a_lo = zt_hi[:, p, h, :], zt_lo[:, p, h, :]
                            nc.tensor.matmul(out_ps[p][:], a_hi, wo_hi[:, h, :], start=(h == 0), stop=False)
                            nc.tensor.matmul(out_ps[p][:], a_hi, wo_lo[:, h, :], start=False, stop=False)
                            last = nc.tensor.matmul(out_ps[p][:], a_lo, wo_hi[:, h, :], start=False, stop=(h == H - 1))
                        last.then_inc(out_full, 1)

                for_pairs(pe, pair)


def ffn_block(nc, T, DM, F, w1_t, w2_t, b1T, b2, x1_dram, out):
    C = DM // P
    FT = F // P
    LAG = 3
    HRING = 4
    with ExitStack() as ctx:
        def sb(name, shape, dt=F32):
            return ctx.enter_context(nc.sbuf_tensor(name, shape, dt))

        def sem(name):
            return ctx.enter_context(nc.semaphore(name))

        x1 = sb("x1", [P, GROUPS, DM])
        x1b = sb("x1b", [P, GROUPS, DM])
        b2_all = sb("b2_all", [P, DM])
        b1_all = sb("b1_all", [P, FT])
        xt_hi = sb("xt_hi", [P, C, BANK], F32R)
        xt_lo = sb("xt_lo", [P, C, BANK], F32R)
        g_t = sb("g_t", [P, 2, BANK])
        h_hi = sb("h_hi", [P, HRING, BANK], F32R)
        h_lo = sb("h_lo", [P, HRING, BANK], F32R)
        r_t = sb("r_t3", [P, GROUPS, DM])
        y_t = sb("y_t", [P, GROUPS, DM])
        ident = sb("ident3", [P, P])
        st = sb("st3", [P, GROUPS, nc.vector.BN_STATS_DIM])
        mv = sb("mv3", [P, GROUPS, nc.vector.BN_AGGR_DIM])
        small = sb("small3", [P, 7, GROUPS])
        var, root, r0, t1, t2, rstd = (small[:, n, :] for n in range(6))
        up = [ctx.enter_context(nc.psum_tensor(f"up{n}", [P, BANK], F32)) for n in range(2)]
        tp = [ctx.enter_context(nc.psum_tensor(f"tp{n}", [P, BANK], F32)) for n in range(2)]
        acc = [ctx.enter_context(nc.psum_tensor(f"acc{n}", [P, DM], F32)) for n in range(GROUPS)]

        bias_loaded = sem("bias_loaded")
        ident_ready = sem("ident_ready")
        x1_loaded = sem("x1_loaded")
        x1b_ready = sem("x1b_ready")
        t_full = sem("t_full")
        t_hi = sem("t_hi")
        t_lo = sem("t_lo")
        up_full = sem("up_full")
        gelu_done = sem("gelu_done")
        h_hi_ready = sem("h_hi_ready")
        h_lo_ready = sem("h_lo_ready")
        acc_full = sem("acc_full")
        r_ready = sem("r_ready3")
        stats_ready = sem("stats_ready")
        aggr_ready = sem("aggr_ready")
        ln_chain = sem("ln_chain3")
        var_ready = sem("var_ready3")
        root_ready = sem("root_ready3")
        y_ready = sem("y_ready")
        y_stored = sem("y_stored")

        x1_v = x1_dram.rearrange("(g i p) d -> g p i d", p=P, i=GROUPS)
        out_v = out.rearrange("(g i p) d -> g p i d", p=P, i=GROUPS)

        def after(eng, s, value, least):
            if least > 0:
                eng.wait_ge(s, value)

        def for_groups(eng, group):
            group(0, 0)
            with eng.Fori(1, GROUPS - 1) as g:
                group(g, 1)
            group(GROUPS - 1, GROUPS - 1)

        with nc.Block() as block:

            @block.sync
            def _(sp):
                sp.dma_start(x1[:], x1_v[0, :, :, :]).then_inc(x1_loaded, 16)
                sp.dma_start(b1_all[:], b1T[:, :]).then_inc(bias_loaded, 16)
                sp.dma_start(b2_all[:], b2.rearrange("(a d) -> a d", a=1).to_broadcast([P, DM])
                             ).then_inc(bias_loaded, 16)

                def group(g, least):
                    if not (isinstance(g, int) and g == GROUPS - 1):
                        sp.wait_ge(t_lo, g * C + C)
                        sp.wait_ge(x1b_ready, g * GROUPS + GROUPS)
                        sp.dma_start(x1[:], x1_v[g + 1, :, :, :]).then_inc(x1_loaded, 16)
                    for i in range(GROUPS):
                        sp.wait_ge(y_ready, g * GROUPS + (i + 1))
                        sp.dma_start(out_v[g, :, i, :], y_t[:, i, :]).then_inc(y_stored, 16)

                for_groups(sp, group)
                sp.wait_ge(y_stored, 16 * GROUPS * GROUPS)

            @block.gpsimd
            def _(pool):
                pool.memset(ident[:], 0.0).then_inc(ident_ready, 1)
                pool.wait_ge(ident_ready, 1)
                pool.affine_select(out=ident[:], in_=ident[:], compare_op=ALU.not_equal, fill=1.0, base=0,
                                   pattern=[[-1, P]], channel_multiplier=1).then_inc(ident_ready, 1)
                pool.wait_ge(bias_loaded, 32)

                def group(g, least):
                    pool.wait_ge(x1_loaded, g * 16 + 16)
                    after(pool, r_ready, g * GROUPS, least)
                    for i in range(GROUPS):
                        last = pool.tensor_tensor(x1b[:, i, :], x1[:, i, :], b2_all[:], ALU.add)
                        last.then_inc(x1b_ready, 1)

                for_groups(pool, group)

            @block.scalar
            def _(act):
                act.wait_ge(bias_loaded, 32)

                def transposed(g):
                    for c in range(C):
                        act.wait_ge(t_full, g * C + (c + 1))
                        nc.scalar.activation(xt_hi[:, c, :], tp[c % 2][:], ACT.Copy).then_inc(t_hi, 1)

                transposed(0)

                def group(g, least):
                    for f in range(FT):
                        act.wait_ge(up_full, g * FT + (f + 1))
                        after(act, h_lo_ready, g * FT + (f - 1), least * FT + f - 1)
                        nc.scalar.activation(g_t[:, f % 2, :], up[f % 2][:], ACT.Gelu, bias=b1_all[:, f:f + 1]
                                             ).then_inc(gelu_done, 1)
                    if not (isinstance(g, int) and g == GROUPS - 1):
                        transposed(g + 1)
                    act.wait_ge(var_ready, g + 1)
                    nc.scalar.activation(root, var, ACT.Sqrt).then_inc(root_ready, 1)

                for_groups(act, group)

            @block.vector
            def _(dve):
                def transposed(g):
                    for c in range(C):
                        dve.wait_ge(t_hi, g * C + (c + 1))
                        dve.tensor_tensor(xt_lo[:, c, :], tp[c % 2][:], xt_hi[:, c, :].bitcast(F32), ALU.subtract
                                          ).then_inc(t_lo, 1)

                transposed(0)

                def group(g, least):
                    for f in range(FT):
                        dve.wait_ge(gelu_done, g * FT + (f + 1))
                        dve.tensor_copy(h_hi[:, f % HRING, :], g_t[:, f % 2, :]).then_inc(h_hi_ready, 1)
                        dve.wait_ge(h_hi_ready, g * FT + (f + 1))
                        dve.tensor_tensor(h_lo[:, f % HRING, :], g_t[:, f % 2, :],
                                          h_hi[:, f % HRING, :].bitcast(F32), ALU.subtract).then_inc(h_lo_ready, 1)
                    if not (isinstance(g, int) and g == GROUPS - 1):
                        transposed(g + 1)
                    dve.wait_ge(x1b_ready, g * GROUPS + GROUPS)
                    after(dve, y_ready, g * GROUPS, least)
                    for i in range(GROUPS):
                        dve.wait_ge(acc_full, g * GROUPS + (i + 1))
                        dve.tensor_tensor(r_t[:, i, :], acc[i][:], x1b[:, i, :], ALU.add).then_inc(r_ready, 1)
                        dve.wait_ge(r_ready, g * GROUPS + (i + 1))
                        dve.bn_stats(st[:, i, :], r_t[:, i, :]).then_inc(stats_ready, 1)
                    dve.wait_ge(stats_ready, g * GROUPS + GROUPS)
                    dve.memset(small[:, 6, :], 0.0)
                    for i in range(GROUPS):
                        dve.bn_aggr(mv[:, i, :], st[:, i, :]).then_inc(aggr_ready, 1)
                    dve.wait_ge(aggr_ready, g * GROUPS + GROUPS)
                    post_norm(nc, dve, mv, var, r0, t1, t2, rstd, GROUPS, ln_chain, g * 5, var_ready, root,
                              root_ready, g)
                    for i in range(GROUPS):
                        after(dve, y_stored, g * 16 * GROUPS, least)
                        dve.tensor_scalar(y_t[:, i, :], r_t[:, i, :], mv[:, i, 0:1], rstd[:, i:i + 1], ALU.subtract,
                                          ALU.mult).then_inc(y_ready, 1)

                for_groups(dve, group)

            @block.tensor
            def _(pe):
                pe.wait_ge(ident_ready, 2)

                def transpose_group(g, least):
                    pe.wait_ge(x1_loaded, g * 16 + 16)
                    for c in range(C):
                        after(pe, t_lo, g * C + (c - 1), least * C + c - 1)
                        for i in range(GROUPS):
                            last = nc.tensor.transpose(tp[c % 2][:, i * P:(i + 1) * P],
                                                       x1[:, i, c * P:(c + 1) * P], ident[:])
                        last.then_inc(t_full, 1)

                def first_product(g, f, least):
                    after(pe, gelu_done, g * FT + (f - 1), least * FT + f - 1)
                    for c in range(C):
                        w = w1_t[:, c, f * P:(f + 1) * P]
                        nc.tensor.matmul(up[f % 2][:], w, xt_hi[:, c, :], start=(c == 0), stop=False)
                        last = nc.tensor.matmul(up[f % 2][:], w, xt_lo[:, c, :], start=False, stop=(c == C - 1))
                    last.then_inc(up_full, 1)

                def second_product(g, f, least):
                    pe.wait_ge(h_lo_ready, g * FT + (f + 1))
                    for i in range(GROUPS):
                        if f == 0:
                            after(pe, r_ready, g * GROUPS + (i + 1 - GROUPS), (least - 1) * GROUPS + i + 1)
                        tok = slice(i * P, (i + 1) * P)
                        nc.tensor.matmul(acc[i][:], h_hi[:, f % HRING, tok], w2_t[:, f, :], start=(f == 0), stop=False)
                        last = nc.tensor.matmul(acc[i][:], h_lo[:, f % HRING, tok], w2_t[:, f, :], start=False,
                                                stop=(f == FT - 1))
                        if f == FT - 1:
                            last.then_inc(acc_full, 1)

                transpose_group(0, 0)

                def group(g, least):
                    pe.wait_ge(t_lo, g * C + C)
                    for f in range(FT):
                        first_product(g, f, least)
                        if f >= LAG:
                            second_product(g, f - LAG, least)
                    if not (isinstance(g, int) and g == GROUPS - 1):
                        transpose_group(g + 1, least + 1)
                    for f in range(FT - LAG, FT):
                        second_product(g, f, least)

                for_groups(pe, group)


def layer(nc, a, out):
    T, DM = a["x"].shape
    H, _, DH = a["wq"].shape
    F = a["b1T"].shape[0] * a["b1T"].shape[1]
    z_dram = nc.dram_tensor("z_scratch", (GROUPS, GROUPS, DH, H, P), F32, kind="Internal").ap()
    x1_dram = nc.dram_tensor("x1_scratch", (T, DM), F32, kind="Internal").ap()
    with ExitStack() as ctx:
        abs_sums = ctx.enter_context(nc.sbuf_tensor("abs_sums", [P, 2, H], F32))
        attention_block(nc, H, T, DM, DH, a["xT"], a["wq"], a["wk"], a["wv"], a["bqkv"],
                        a["w1"], a["w2T"], abs_sums, z_dram)
        w1_t = ctx.enter_context(nc.sbuf_tensor("w1_t", [P, DM // P, F], F32R))
        w2_t = ctx.enter_context(nc.sbuf_tensor("w2_t", [P, F // P, DM], F32R))
        projection_block(nc, H, T, DM, F, a["x"], a["wo"], a["bo"], a["w1T"], a["w2T"], abs_sums, w1_t, w2_t,
                         z_dram, x1_dram)
        ffn_block(nc, T, DM, F, w1_t, w2_t, a["b1T"], a["b2"], x1_dram, out)


def kernel(**inputs):
    import numpy as np
    import concourse.bacc as bacc
    from concourse.bass_utils import run_bass_kernel_spmd

    def get(name):
        return np.asarray(inputs["L0_" + name])

    x = get("attn_x")[0]
    w1, w2 = get("ffn_w1"), get("ffn_w2")
    F, DM = w1.shape
    arrays = {
        "x": x, "xT": x.T,
        "wq": get("attn_W_Q"), "wk": get("attn_W_K"), "wv": get("attn_W_V"), "wo": get("attn_W_O"),
        "bqkv": np.stack([get("attn_b_Q"), get("attn_b_K"), get("attn_b_V")], axis=-1), "bo": get("attn_b_O"),
        "w1": w1, "w1T": w1.T.reshape(DM // P, P, 2, F // 2).transpose(0, 2, 1, 3).reshape(-1, P, F // 2),
        "w2T": w2.T, "b1T": get("ffn_b1").reshape(F // P, P).T, "b2": get("ffn_b2"),
    }
    arrays = {n: np.ascontiguousarray(v) for n, v in arrays.items()}
    nc = bacc.Bacc("TRN2", target_bir_lowering=False, num_devices=1)
    aps = {n: nc.dram_tensor("in_" + n, v.shape, mybir.dt.from_np(v.dtype), kind="ExternalInput").ap()
           for n, v in arrays.items()}
    out = nc.dram_tensor("out", x.shape, F32, kind="ExternalOutput").ap()
    layer(nc, aps, out)
    r = run_bass_kernel_spmd(nc, [{"in_" + n: v for n, v in arrays.items()}], core_ids=[0])
    return r.results[0]["out"].reshape(1, *x.shape)
```

```python
from contextlib import ExitStack

import concourse.bass as bass
from concourse import mybir

F32 = mybir.dt.float32
F32R = mybir.dt.float32r
BF16 = mybir.dt.bfloat16
ALU = mybir.AluOpType
ACT = mybir.ActivationFunctionType
AX_X = mybir.AxisListType.X

P = 128
BANK = 512
EPS = 1e-5
MASKED = -1.0e5

GROUPS = 4
RING = 3
SRING = 4
PTRING = 4
UNITS = 60
KTS = 40
EVENTS = 40
CARRY_U = 17
CARRY_K = 16


def event(g, j, b):
    return sum(4 * (n + 1) for n in range(g)) + j * (g + 1) + b


def head_order(first):
    items, u, m = [], 0, 0
    for g in range(GROUPS):
        gp = (g - 1) % GROUPS
        carried = -EVENTS if g == 0 else 0
        prev = not (first and g == 0)
        tail = [("exp", gp, 3, b, event(gp, 3, b) + carried) for b in range(gp + 1)] if prev else []
        items += tail[:2]
        items.append(("q", g, u)); u += 1
        items += tail[2:3]
        items.append(("k", g, u)); u += 1
        items += tail[3:]
        items.append(("vt", g, u)); u += 1
        m0 = m
        pend = []
        for j in range(GROUPS):
            kts = [j * (gp + 1) + n for n in range(gp + 1)] if prev else []
            exps = [("exp", g, j - 1, b, event(g, j - 1, b)) for b in range(g + 1)] if j else []
            for b in range(g + 1):
                for _ in range(min(len(kts), 2 if b == 0 else 1)):
                    kt = kts.pop(0)
                    items.append(("kt", gp, kt, u, m, carried)); pend.append((kt, u, m)); u += 1; m += 1
                    items += exps[:1]; del exps[:1]
                    if len(pend) > 2:
                        items.append(("pv", gp) + pend.pop(0))
                while exps and exps[0][4] <= event(g, j, b) - SRING:
                    items.append(exps.pop(0))
                items.append(("s", g, j, b, event(g, j, b)))
            for kt in kts:
                items.append(("kt", gp, kt, u, m, carried)); pend.append((kt, u, m)); u += 1; m += 1
                items += exps[:1]; del exps[:1]
                if len(pend) > 2:
                    items.append(("pv", gp) + pend.pop(0))
            items += exps
            if j == 1 and prev:
                items.append(("sum", gp, carried))
        items.append(("v", g, u)); u += 1
        items += [("pv", gp) + x for x in pend]
        if prev:
            items.append(("norm", gp, u, g)); u += 1
    return items


def tail_order():
    gp, items, pend = GROUPS - 1, [], []
    items += [("exp", gp, 3, b, event(gp, 3, b) - EVENTS) for b in range(gp + 1)]
    items.append(("sum", gp, -EVENTS))
    for kt in range(4 * (gp + 1)):
        items.append(("kt", gp, kt, kt, kt, -EVENTS)); pend.append((kt, kt, kt))
        if len(pend) > 2:
            items.append(("pv", gp) + pend.pop(0))
    items += [("pv", gp) + x for x in pend]
    items.append(("norm", gp, 4 * (gp + 1), 0))
    return items


class Map:
    ZONES = {"x": 64, "w": 18, "even": 24, "k": 16, "v": 16, "odd": 32, "pt": 16, "q": 16, "own": 5}

    def __init__(self, nc):
        self.nc, self.next = nc, {}
        at = -(-nc.sbuf_base // 64) * 64
        for zone, kib in self.ZONES.items():
            self.next[zone] = at
            at += kib * 1024
        self.start = dict(self.next)
        assert at <= nc.sbuf_usable_end

    def stage(self):
        self.next = {z: self.next[z] if z == "own" else a for z, a in self.start.items()}

    def put(self, zone, name, shape, dt=F32):
        size = 2 if dt == BF16 else 4
        for n in shape[1:]:
            size *= n
        t = self.nc.alloc_sbuf_tensor_at(name, shape, dt, offset=self.next[zone])
        self.next[zone] += -(-size // 32) * 32
        return t


def attention_stage(nc, sem, sbuf, banks, ident, H, T, DM, DH, xT, wq, wk, wv, bqkv, f1, f2, abs_sums, z_dram):
    C = DM // P
    SCALE = float(DH) ** -0.5
    NEG = MASKED / SCALE
    assert DH == P and T == GROUPS * BANK and C == 4
    sb = sbuf.put

    x_hi = sb("x", "x_hi", [P, C, T], F32R)
    x_lo = sb("x", "x_lo", [P, C, T], F32R)
    k_hi = sb("k", "k_hi", [P, T], F32R)
    k_lo = sb("k", "k_lo", [P, T], F32R)
    v_hi = sb("v", "v_hi", [P, T], F32R)
    v_lo = sb("v", "v_lo", [P, T], F32R)
    q_hi = sb("q", "q_hi", [P, BANK], F32R)
    q_lo = sb("q", "q_lo", [P, BANK], F32R)
    vt = sb("q", "vt", [P, BANK])
    probs_even = sb("even", "probs_even", [P, GROUPS, 3 * BANK])
    probs_odd = sb("odd", "probs_odd", [P, GROUPS, 4 * BANK])
    pt_hi = sb("pt", "pt_hi", [P, PTRING, BANK], F32R)
    pt_lo = sb("pt", "pt_lo", [P, PTRING, BANK], F32R)
    z_raw = sb("q", "z_raw", [P, BANK])
    z_out = sb("q", "z_out", [P, 2, BANK])
    w_raw = sb("w", "w_raw", [P, 3, C, DH])
    w_hi = sb("w", "w_hi", [P, 3, C, DH], F32R)
    w_lo = sb("w", "w_lo", [P, 3, C, DH], F32R)
    b_raw = sb("own", "b_raw", [P, 4])
    b_cur = sb("own", "b_cur", [P, 4])
    zeros = sb("own", "zeros", [P, 4])
    ident_bf = sb("own", "ident_bf", [P, P], BF16)
    mask_bf = sb("own", "mask_bf", [P, P], BF16)
    f_raw = sb("q", "f_raw", [P, 2, DM])
    mx = sb("own", "mx", [P, 2, GROUPS])
    mx_scaled = sb("own", "mx_scaled", [P, GROUPS])
    neg_max = sb("own", "neg_max", [P, 2, GROUPS])
    sums = sb("own", "sums", [P, 2, GROUPS, GROUPS])
    total = sb("own", "total", [P, GROUPS])
    rinv = sb("own", "rinv", [P, GROUPS])
    probs = [probs_even, probs_odd]

    score, ring, z_ps = banks[0:SRING], banks[SRING:SRING + RING], banks[SRING + RING]

    x_loaded = [sem(f"x_loaded{g}") for g in range(GROUPS)]
    x_hi_ready = sem("x_hi_ready")
    x_lo_ready = sem("x_lo_ready")
    w_loaded = sem("w_loaded")
    w_part = sem("w_part")
    w_ready = sem("w_ready")
    consts = sem("consts")
    ring_full = sem("ring_full")
    ring_hi = sem("ring_hi")
    ring_lo = sem("ring_lo")
    score_full = sem("score_full")
    max_part = sem("max_part")
    max_ready = sem("max_ready")
    exp_done = sem("exp_done")
    sum_part = sem("sum_part")
    rinv_ready = sem("rinv_ready")
    z_stored = [sem(f"z_stored{n}") for n in range(2)]
    f_loaded = sem("f_loaded")
    f_summed = sem("f_summed")

    def count(eng, s, per_head, h, n):
        if isinstance(h, int):
            if h * per_head + n > 0:
                eng.wait_ge(s, h * per_head + n)
        else:
            assert per_head + n > 0
            eng.wait_ge(s, h * per_head + n)

    def bank(first, u):
        return (u if first else u - CARRY_U) % RING

    def slot(first, m):
        return (m if first else m - CARRY_K) % PTRING

    def for_heads(eng, run):
        run(0, head_order(True), True)
        with eng.Fori(1, H) as h:
            run(h, head_order(False), False)
        run(H, tail_order(), False)

    LAST_VT = [it[2] for it in head_order(False) if it[0] == "vt"][-1] - CARRY_U
    last_vt = (H - 1) * UNITS + LAST_VT + 1


    def sync(sp, before_norm):
        for g in range(GROUPS):
            blk = slice(g * BANK, (g + 1) * BANK)
            if g == 1:
                sp.wait_ge(w_loaded, 64)
            sp.dma_start(probs_odd[:, :, blk], xT.rearrange("(c p) t -> p c t", p=P)[:, :, blk]
                         ).then_inc(x_loaded[g], 16)

        f1_v, f2_v = (f.rearrange("(n p) d -> n p d", p=P) for f in (f1, f2))

        def load_ffn_slices(h):
            for n, f in enumerate((f1_v, f2_v)):
                count(sp, f_summed, 2, h, 0)
                sp.dma_start(f_raw[:, n, :], f[h, :, :]).then_inc(f_loaded, 16)

        def run(h, order, first):
            for it in order:
                if it[0] == "norm":
                    _, gp, u, n = it
                    hz = h - 1 if gp == GROUPS - 1 else h
                    count(sp, ring_lo, UNITS, h, u + 1 - (0 if first else CARRY_U))
                    slot_z = gp % 2
                    sp.dma_start(z_dram[gp, :, :, hz, :].rearrange("i e q -> e i q"),
                                 z_out[:, slot_z, :].rearrange("e (i q) -> e i q", q=P)
                                 ).then_inc(z_stored[slot_z], 16)

        def run_last(h, order, first):
            run(h, order[:-1], first)
            sp.wait_ge(ring_lo, last_vt)
            before_norm(sp)
            run(h, order[-1:], first)

        load_ffn_slices(0)
        run(0, head_order(True), True)
        with sp.Fori(1, H - 1) as h:
            load_ffn_slices(h)
            run(h, head_order(False), False)
        load_ffn_slices(H - 1)
        run_last(H - 1, head_order(False), False)
        run(H, tail_order(), False)

    def gpsimd(pool):
        pool.memset(ident[:], 0.0).then_inc(consts, 1)
        pool.memset(ident_bf[:], 0.0).then_inc(consts, 1)
        pool.memset(mask_bf[:], 0.0).then_inc(consts, 1)
        pool.memset(zeros[:], 0.0).then_inc(consts, 1)
        pool.wait_ge(consts, 4)
        for m in (ident, ident_bf):
            pool.affine_select(out=m[:], in_=m[:], compare_op=ALU.not_equal, fill=1.0, base=0,
                               pattern=[[-1, P]], channel_multiplier=1).then_inc(consts, 1)
        pool.affine_select(out=mask_bf[:], in_=mask_bf[:], compare_op=ALU.is_ge, fill=NEG, base=0,
                           pattern=[[-1, P]], channel_multiplier=1).then_inc(consts, 1)

        def load(h):
            for n, w in enumerate((wq, wk, wv)):
                pool.dma_start(w_raw[:, n, :, :], w[h, :, :].rearrange("(c p) e -> p c e", p=P)
                               ).then_inc(w_loaded, 16)
            pool.dma_start(b_raw[:, 0:3], bqkv[h, :, :]).then_inc(w_loaded, 16)

        def split(h):
            pool.wait_ge(w_loaded, h * 64 + 64)
            pool.tensor_tensor(b_cur[:, 0:3], b_raw[:, 0:3], zeros[:, 0:3], ALU.add).then_inc(w_part, 1)
            for n in range(3):
                pool.tensor_scalar(w_hi[:, n, :, :], w_raw[:, n, :, :], 1.0, 0.0, ALU.mult, ALU.add
                                   ).then_inc(w_part, 1)
            for n in range(3):
                pool.wait_ge(w_part, h * 6 + (n + 2))
                last = pool.tensor_tensor(w_lo[:, n, :, :], w_raw[:, n, :, :],
                                          w_hi[:, n, :, :].bitcast(F32), ALU.subtract)
                last.then_inc(w_part if n < 2 else w_ready, 1)

        load(0)
        split(0)
        with pool.Fori(1, H) as h:
            pool.wait_ge(w_part, h * 6)
            pool.wait_ge(w_ready, h)
            load(h)
            pool.wait_ge(ring_lo, (h - 1) * UNITS + (LAST_VT + 1))
            split(h)

    def scalar(act):
        def hi_part(out, src, bias=None):
            if bias is None:
                return nc.scalar.activation(out, src, ACT.Copy)
            return nc.scalar.activation(out, src, ACT.Identity, bias=bias)

        for g in range(GROUPS):
            blk = slice(g * BANK, (g + 1) * BANK)
            act.wait_ge(x_loaded[g], 16)
            hi_part(x_hi[:, :, blk], probs_odd[:, :, blk]).then_inc(x_hi_ready, 1)

        def run(h, order, first):
            off = 0 if first else CARRY_U
            for it in order:
                kind, g = it[0], it[1]
                if kind in ("q", "k", "vt", "v"):
                    u = it[2]
                    src = ring[bank(first, u)]
                    count(act, ring_full, UNITS, h, u + 1 - off)
                    if kind == "q":
                        i = hi_part(q_hi[:], src[:], b_cur[:, 0:1])
                    elif kind == "k":
                        i = hi_part(k_hi[:, g * BANK:(g + 1) * BANK], src[:], b_cur[:, 1:2])
                    elif kind == "vt":
                        i = hi_part(vt[:, 0:BANK // 2], src[:, 0:BANK // 2], b_cur[:, 2:3])
                    else:
                        i = hi_part(v_hi[:, g * BANK:(g + 1) * BANK], src[:])
                    i.then_inc(ring_hi, 1)
                elif kind == "kt":
                    _, _, kt, u, m, _ = it
                    c0 = max(0, kt - 4 * g) * P
                    count(act, ring_full, UNITS, h, u + 1 - off)
                    hi_part(pt_hi[:, slot(first, m), c0:], ring[bank(first, u)][:, c0:]
                            ).then_inc(ring_hi, 1)
                elif kind == "norm":
                    u = it[2]
                    count(act, ring_full, UNITS, h, u + 1 - off)
                    hi_part(z_raw[:], z_ps[:]).then_inc(ring_hi, 1)
                elif kind == "exp":
                    _, _, j, b, e = it
                    w = P * (j + 1) if b == g else BANK
                    hh = 4 * g + j + 1 - (16 if e < 0 else 0)
                    count(act, max_ready, 4 * GROUPS, h, hh)
                    nc.scalar.activation(probs[g % 2][:, j, b * BANK:b * BANK + w],
                                         score[e % SRING][:, 0:w], ACT.Exp,
                                         bias=neg_max[:, g % 2, j:j + 1], scale=SCALE,
                                         accum_out=sums[:, g % 2, j, b:b + 1]).then_inc(exp_done, 1)

        for_heads(act, run)

    def vector(dve):
        for g in range(GROUPS):
            blk = slice(g * BANK, (g + 1) * BANK)
            dve.wait_ge(x_hi_ready, g + 1)
            dve.tensor_tensor(x_lo[:, :, blk], probs_odd[:, :, blk], x_hi[:, :, blk].bitcast(F32),
                              ALU.subtract).then_inc(x_lo_ready, 1)

        def run(h, order, first):
            off = 0 if first else CARRY_U
            for it in order:
                kind, g = it[0], it[1]
                if kind in ("q", "k", "vt", "v"):
                    u = it[2]
                    src = ring[bank(first, u)]
                    blk = slice(g * BANK, (g + 1) * BANK)
                    count(dve, ring_hi, UNITS, h, u + 1 - off)
                    if kind == "q":
                        i = dve.scalar_tensor_tensor(out=q_lo[:], in0=src[:], scalar=b_cur[:, 0:1],
                                                     in1=q_hi[:].bitcast(F32), op0=ALU.add,
                                                     op1=ALU.subtract)
                    elif kind == "k":
                        i = dve.scalar_tensor_tensor(out=k_lo[:, blk], in0=src[:], scalar=b_cur[:, 1:2],
                                                     in1=k_hi[:, blk].bitcast(F32), op0=ALU.add,
                                                     op1=ALU.subtract)
                    elif kind == "vt":
                        i = dve.tensor_scalar(vt[:, BANK // 2:], src[:, BANK // 2:], b_cur[:, 2:3], None,
                                              ALU.add)
                    else:
                        i = dve.tensor_tensor(v_lo[:, blk], src[:], v_hi[:, blk].bitcast(F32),
                                              ALU.subtract)
                    i.then_inc(ring_lo, 1)
                elif kind == "kt":
                    _, _, kt, u, m, _ = it
                    c0 = max(0, kt - 4 * g) * P
                    s = slot(first, m)
                    count(dve, ring_hi, UNITS, h, u + 1 - off)
                    dve.tensor_tensor(pt_lo[:, s, c0:], ring[bank(first, u)][:, c0:],
                                      pt_hi[:, s, c0:].bitcast(F32), ALU.subtract).then_inc(ring_lo, 1)
                elif kind == "norm":
                    _, gp, u, n = it
                    stores = gp // 2 - (2 if gp == GROUPS - 1 else 0)
                    count(dve, z_stored[gp % 2], 16 * 2, h, 16 * stores)
                    count(dve, ring_hi, UNITS, h, u + 1 - off)
                    dve.tensor_tensor(z_out[:, gp % 2, :], ring[bank(first, u)][:], z_raw[:],
                                      ALU.mult).then_inc(ring_lo, 1)
                elif kind == "s":
                    _, _, j, b, e = it
                    w = P * (j + 1) if b == g else BANK
                    count(dve, score_full, EVENTS, h, e + 1)
                    dve.tensor_reduce(mx[:, j % 2, b:b + 1], score[e % SRING][:, 0:w], AX_X, ALU.max
                                      ).then_inc(max_part, 1)
                    if b == g:
                        count(dve, max_part, EVENTS, h, e + 1)
                        dve.tensor_scalar(mx_scaled[:, 0:g + 1], mx[:, j % 2, 0:g + 1], -SCALE, None,
                                          ALU.mult, ALU.min, accum_out=neg_max[:, g % 2, j:j + 1]
                                          ).then_inc(max_ready, 1)
                elif kind == "sum":
                    _, _, carried = it
                    n_sum = g + 1 - (GROUPS if carried else 0)
                    count(dve, exp_done, EVENTS, h, event(g, 3, g) + 1 + carried)
                    dve.tensor_reduce(total[:], sums[:, g % 2, :, 0:g + 1], AX_X, ALU.add
                                      ).then_inc(sum_part, 1)
                    count(dve, sum_part, GROUPS, h, n_sum)
                    dve.reciprocal(rinv[:], total[:]).then_inc(rinv_ready, 1)
                    if g < 2:
                        dve.wait_ge(f_loaded, h * 32 + 32)
                        column = abs_sums[:, g, bass.ds(h, 1)] if not isinstance(h, int) \
                            else abs_sums[:, g, h:h + 1]
                        dve.tensor_reduce(column, f_raw[:, g, :], AX_X, ALU.add,
                                          apply_absolute_value=True).then_inc(f_summed, 1)

        for_heads(dve, run)

    def tensor(pe):
        pe.wait_ge(consts, 7)

        def project(out, n, g):
            blk = slice(g * BANK, (g + 1) * BANK)
            for c in range(C):
                nc.tensor.matmul(out, w_hi[:, n, c, :], x_hi[:, c, blk], start=(c == 0), stop=False)
                nc.tensor.matmul(out, w_hi[:, n, c, :], x_lo[:, c, blk], start=False, stop=False)
                last = nc.tensor.matmul(out, w_lo[:, n, c, :], x_hi[:, c, blk], start=False,
                                        stop=(c == C - 1))
            return last

        def run(h, order, first):
            off = 0 if first else CARRY_U
            for it in order:
                kind, g = it[0], it[1]
                if kind in ("q", "k", "vt", "v"):
                    u = it[2]
                    out = ring[bank(first, u)]
                    if kind == "q" and g == 0:
                        pe.wait_ge(w_ready, h + 1)
                    if kind == "q" and first:
                        pe.wait_ge(x_lo_ready, g + 1)
                    count(pe, ring_lo, UNITS, h, u - RING + 1 - off)
                    if kind == "v":
                        u_vt = [x[2] for x in order if x[0] == "vt" and x[1] == g][0]
                        count(pe, ring_lo, UNITS, h, u_vt + 1 - off)
                        for t in range(GROUPS):
                            last = nc.tensor.transpose(out[:, t * P:(t + 1) * P],
                                                       vt[:, t * P:(t + 1) * P], ident[:])
                    else:
                        last = project(out[:], ("q", "k", "vt").index(kind), g)
                    last.then_inc(ring_full, 1)
                elif kind == "kt":
                    _, _, kt, u, m, carried = it
                    count(pe, ring_lo, UNITS, h, u - RING + 1 - off)
                    count(pe, exp_done, EVENTS, h, event(g, 3, kt // 4) + 1 + carried)
                    for j in range(max(0, kt - 4 * g), GROUPS):
                        last = nc.tensor.transpose(ring[bank(first, u)][:, j * P:(j + 1) * P],
                                                   probs[g % 2][:, j, kt * P:(kt + 1) * P], ident[:])
                    last.then_inc(ring_full, 1)
                elif kind == "pv":
                    _, _, kt, u, m = it
                    c0 = max(0, kt - 4 * g) * P
                    s = slot(first, m)
                    vs = slice(kt * P, (kt + 1) * P)
                    end = kt == 4 * g + 3
                    count(pe, ring_lo, UNITS, h, u + 1 - off)
                    nc.tensor.matmul(z_ps[:, c0:], v_hi[:, vs], pt_hi[:, s, c0:], start=(kt == 0), stop=False)
                    nc.tensor.matmul(z_ps[:, c0:], v_hi[:, vs], pt_lo[:, s, c0:], start=False, stop=False)
                    nc.tensor.matmul(z_ps[:, c0:], v_lo[:, vs], pt_hi[:, s, c0:], start=False, stop=end)
                elif kind == "norm":
                    _, gp, u, n = it
                    count(pe, ring_lo, UNITS, h, u - RING + 1 - off)
                    count(pe, rinv_ready, GROUPS, h, gp + 1 - (GROUPS if gp == GROUPS - 1 else 0))
                    for j in range(GROUPS):
                        last = nc.tensor.transpose(ring[bank(first, u)][:, j * P:(j + 1) * P],
                                                   rinv[:, j:j + 1].to_broadcast([P, P]), ident[:])
                    last.then_inc(ring_full, 1)
                elif kind == "s":
                    _, _, j, b, e = it
                    w = P * (j + 1) if b == g else BANK
                    keys = slice(b * BANK, b * BANK + w)
                    out = score[e % SRING][:, 0:w]
                    qs = slice(j * P, (j + 1) * P)
                    if j == 0 and b == 0:
                        u = [x[2] for x in order if x[0] == "k" and x[1] == g][0]
                        count(pe, ring_lo, UNITS, h, u + 1 - off)
                    count(pe, exp_done, EVENTS, h, e - SRING + 1)
                    nc.tensor.matmul(out, q_hi[:, qs], k_hi[:, keys], start=True, stop=False)
                    nc.tensor.matmul(out, q_hi[:, qs], k_lo[:, keys], start=False, stop=False)
                    last = nc.tensor.matmul(out, q_lo[:, qs], k_hi[:, keys], start=False, stop=(b < g))
                    if b == g:
                        last = nc.tensor.matmul(out[:, w - P:w], ident_bf[:], mask_bf[:], start=False,
                                                stop=True)
                    last.then_inc(score_full, 1)

        for_heads(pe, run)

    return dict(
        sync=sync, gpsimd=gpsimd, scalar=scalar, vector=vector, tensor=tensor, ring_lo=ring_lo,
        z_stored=z_stored, f_summed=f_summed,
        last_vt=last_vt, all_heads_units=UNITS * H - CARRY_U, stores=16 * GROUPS * H // 2,
        group_stored=lambda g: (z_stored[g % 2], 16 * (2 * (H - 1) + g // 2 + 1)))


def post_norm(nc, dve, var, r0, t1, t2, rstd, chain, base, root, root_ready, turn):
    dve.wait_ge(root_ready, turn)
    dve.reciprocal(r0, root).then_inc(chain, 1)
    dve.wait_ge(chain, base + 1)
    dve.tensor_tensor(t1, r0, r0, ALU.mult).then_inc(chain, 1)
    dve.wait_ge(chain, base + 2)
    dve.tensor_tensor(t2, t1, var, ALU.mult).then_inc(chain, 1)
    dve.wait_ge(chain, base + 3)
    dve.tensor_scalar(t1, t2, -0.5, 1.5, ALU.mult, ALU.add).then_inc(chain, 1)
    dve.wait_ge(chain, base + 4)
    dve.tensor_tensor(rstd, t1, r0, ALU.mult).then_inc(chain, 1)
    dve.wait_ge(chain, base + 5)


def projection_stage(nc, sem, sbuf, banks, before, H, T, DM, F, x, wo, bo, w1T, w2T, abs_sums, w1_t, w2_t, z_dram,
                     x1_dram):
    TILES = T // P
    PAIRS = TILES // 2
    HALF = F * (DM // P) // PAIRS
    WO_PARTS = 8
    HP = H // WO_PARTS
    sb = sbuf.put

    wo_hi = sb("x", "wo_hi", [P, H, DM], F32R)
    wo_lo = sb("x", "wo_lo", [P, H, DM], F32R)
    wo_raw = sb("w", "wo_raw", [P, 2, HP, DM])
    zt_raw = sb("w", "zt_raw", [P, H, P])
    zt_hi = [None, None]
    zt_lo = [None, None]
    zt_hi[0] = sb("even", "zt_hi0", [P, H, P], F32R)
    zt_lo[0] = sb("even", "zt_lo0", [P, H, P], F32R)
    zt_hi[1] = sb("even", "zt_hi1", [P, H, P], F32R)
    zt_lo[1] = sb("k", "zt_lo1", [P, H, P], F32R)
    x_t = sb("k", "x_t", [P, 2, DM])
    xb_t = sb("k", "xb_t", [P, 2, DM])
    bo_all = sb("w", "bo_all", [P, DM])
    r_t = sb("q", "r_t", [P, DM])
    x1_t = sb("q", "x1_t", [P, 2, DM])
    below = sb("q", "below", [P, HALF], BF16)
    f_raw = sb("q", "f_raw2", [P, HALF])
    ones = sb("own", "ones", [P, P])
    sums = sb("own", "sums2", [P, 2])
    thr = sb("own", "thr", [P, 2])
    neg_thr = sb("own", "neg_thr", [P, 2])
    st = sb("own", "st", [P, nc.vector.BN_STATS_DIM])
    mv = sb("own", "mv", [P, 1, nc.vector.BN_AGGR_DIM])
    small = sb("own", "small", [P, 8])
    var, root, r0, t1, t2, rstd = (small[:, n:n + 1] for n in range(6))
    out_ps = banks[0:2]
    sum_ps = banks[2][:, 0:2]

    wo_loaded = [sem(f"wo_loaded{n}") for n in range(2)]
    wo_hi_ready = sem("wo_hi_ready")
    wo_lo_ready = sem("wo_lo_ready")
    z_loaded = sem("z_loaded")
    z_hi_ready = sem("z_hi_ready")
    z_lo_ready = sem("z_lo_ready")
    x_loaded = [sem(f"x_loaded_s{n}") for n in range(2)]
    bo_loaded = sem("bo_loaded")
    xb_ready = sem("xb_ready")
    out_full = sem("out_full")
    r_ready = sem("r_ready")
    ln_step = sem("ln_step")
    ln_chain = sem("ln_chain")
    var_ready = sem("var_ready")
    root_ready = sem("root_ready")
    x1_ready = sem("x1_ready")
    x1_stored = [sem(f"x1_stored{n}") for n in range(2)]
    f_loaded = sem("f_loaded2")
    below_ready = sem("below_ready")
    ternary = sem("ternary")
    ones_ready = sem("ones_ready")
    sums_ready = sem("sums_ready")
    total_ready = sem("total_ready")
    scale_ready = sem("scale_ready")
    thr_ready = sem("thr_ready")

    x_v = x.rearrange("(i p) d -> i p d", p=P)
    x1_v = x1_dram.rearrange("(i p) d -> i p d", p=P)
    wo_v = wo.rearrange("h e d -> e h d")
    w2_v = w2T.rearrange("(n a p) d -> n p a d", p=P, a=HALF // DM)
    w1_flat = w1_t[:].rearrange("p c f -> p (c f)")
    w2_flat = w2_t[:].rearrange("p c d -> p (c d)")

    def after(eng, s, value, least):
        if least > 0:
            eng.wait_ge(s, value)

    def for_pairs(eng, pair, before_last=None):
        pair(0, 0)
        with eng.Fori(1, PAIRS - 1) as it:
            pair(it, 1)
        pair(PAIRS - 1, PAIRS - 1, before_last)


    def load_z(sp, i, least):
        after(sp, z_lo_ready, i, least)
        sp.dma_start(zt_raw[:], z_dram.rearrange("g i e h q -> (g i) e h q")[i, :, :, :]
                     ).then_inc(z_loaded, 16)

    def first_loads(sp):
        for n in range(WO_PARTS):
            if n >= 2:
                sp.wait_ge(wo_lo_ready, n - 1)
            sp.dma_start(wo_raw[:, n % 2, :, :], wo_v[:, n * HP:(n + 1) * HP, :]
                         ).then_inc(wo_loaded[n % 2], 16)
            if n == 1:
                sp.wait_ge(*before["group_stored"](0))
                load_z(sp, 0, 0)

    def sync(sp, before_last):
        sp.dma_start(bo_all[:], bo.rearrange("(a d) -> a d", a=1).to_broadcast([P, DM])
                     ).then_inc(bo_loaded, 16)
        sp.wait_ge(before["ring_lo"], before["all_heads_units"])
        for s in before["z_stored"]:
            sp.wait_ge(s, before["stores"])
        sp.wait_ge(before["f_summed"], 2 * H)

        def pair(it, least, before_last=None):
            for p in range(2):
                if p == 1 and before_last:
                    before_last()
                i = it * 2 + p
                if not (isinstance(it, int) and i == TILES - 1):
                    load_z(sp, i + 1, 2 * least + p + 1)
                after(sp, xb_ready, i - 1, 2 * least + p - 1)
                sp.dma_start(x_t[:, p, :], x_v[i, :, :]).then_inc(x_loaded[p], 16)
                after(sp, ternary, i, 2 * least + p)
                if p == 0:
                    sp.dma_start(f_raw[:], w1T[it, :, :]).then_inc(f_loaded, 16)
                else:
                    sp.dma_start(f_raw[:].rearrange("p (a d) -> p a d", d=DM), w2_v[it, :, :, :]
                                 ).then_inc(f_loaded, 16)

        for_pairs(sp, pair, before_last)

    def gpsimd(pool):
        def split(hi, lo, raw, hi_ready, lo_ready, count):
            pool.tensor_scalar(hi, raw, 1.0, 0.0, ALU.mult, ALU.add).then_inc(hi_ready, 1)
            pool.wait_ge(hi_ready, count)
            pool.tensor_tensor(lo, raw, hi.bitcast(F32), ALU.subtract).then_inc(lo_ready, 1)

        pool.wait_ge(before["ring_lo"], before["last_vt"])
        for n in range(WO_PARTS):
            pool.wait_ge(wo_loaded[n % 2], 16 * (n // 2 + 1))
            hs = slice(n * HP, (n + 1) * HP)
            split(wo_hi[:, hs, :], wo_lo[:, hs, :], wo_raw[:, n % 2, :, :], wo_hi_ready, wo_lo_ready, n + 1)
        pool.wait_ge(before["ring_lo"], before["all_heads_units"])
        pool.wait_ge(z_loaded, 16)
        split(zt_hi[0][:], zt_lo[0][:], zt_raw[:], z_hi_ready, z_lo_ready, 1)
        pool.wait_ge(bo_loaded, 16)

        def pair(it, least, before_last=None):
            for p in range(2):
                if p == 1 and before_last:
                    before_last()
                i = it * 2 + p
                pool.wait_ge(x_loaded[p], it * 16 + 16)
                after(pool, r_ready, i - 1, 2 * least + p - 1)
                pool.tensor_tensor(xb_t[:, p, :], x_t[:, p, :], bo_all[:], ALU.add).then_inc(xb_ready, 1)

        for_pairs(pool, pair)

    def scalar(act, before_last):
        def z_part(i, p):
            act.wait_ge(z_loaded, i * 16 + 16)
            nc.scalar.activation(zt_hi[p][:], zt_raw[:], ACT.Copy).then_inc(z_hi_ready, 1)

        def pair(it, least, before_last=None):
            for p in range(2):
                if p == 1 and before_last:
                    before_last()
                i = it * 2 + p
                if not (isinstance(it, int) and i == TILES - 1):
                    after(act, out_full, i, 2 * least + p)
                    z_part(i + 1, 1 - p)
                act.wait_ge(var_ready, i + 1)
                nc.scalar.activation(root, var, ACT.Sqrt).then_inc(root_ready, 1)
                act.wait_ge(x1_ready, i + 1)
                act.dma_start(x1_v[i, :, :], x1_t[:, p, :]).then_inc(x1_stored[p], 16)

        for_pairs(act, pair, before_last)

    def vector(dve, before_last):
        def z_part(i, p):
            dve.wait_ge(z_hi_ready, i + 1)
            dve.tensor_tensor(zt_lo[p][:], zt_raw[:], zt_hi[p][:].bitcast(F32), ALU.subtract
                              ).then_inc(z_lo_ready, 1)

        dve.memset(ones[:], 1.0).then_inc(ones_ready, 1)
        dve.tensor_reduce(sums[:], abs_sums[:], AX_X, ALU.add).then_inc(sums_ready, 1)
        dve.wait_ge(total_ready, 1)
        dve.tensor_scalar(thr[:], sum_ps, 1.0 / (F * DM), 0.7, ALU.mult, ALU.mult).then_inc(scale_ready, 1)
        dve.wait_ge(scale_ready, 1)
        dve.tensor_scalar(neg_thr[:], thr[:], -1.0, None, ALU.mult).then_inc(thr_ready, 1)
        dve.wait_ge(thr_ready, 1)

        def pair(it, least, before_last=None):
            for p in range(2):
                if p == 1 and before_last:
                    before_last()
                i = it * 2 + p
                if not (isinstance(it, int) and i == TILES - 1):
                    z_part(i + 1, 1 - p)
                dve.wait_ge(out_full, i + 1)
                dve.wait_ge(xb_ready, i + 1)
                after(dve, x1_ready, i, 2 * least + p)
                dve.tensor_tensor(r_t[:], out_ps[p][:], xb_t[:, p, :], ALU.add).then_inc(r_ready, 1)
                dve.wait_ge(r_ready, i + 1)
                dve.bn_stats(st[:], r_t[:]).then_inc(ln_step, 1)
                dve.wait_ge(f_loaded, i * 16 + 16)
                dve.tensor_scalar(below[:], f_raw[:], neg_thr[:, p:p + 1], None, ALU.is_le
                                  ).then_inc(below_ready, 1)
                dve.wait_ge(ln_step, i * 2 + 1)
                dve.wait_ge(below_ready, i + 1)
                flat = (w1_flat, w2_flat)[p]
                dve.scalar_tensor_tensor(out=flat[:, bass.ds(it * HALF, HALF)], in0=f_raw[:],
                                         scalar=thr[:, p:p + 1], in1=below[:], op0=ALU.is_ge,
                                         op1=ALU.subtract).then_inc(ternary, 1)
                dve.bn_aggr(mv[:, 0, :], st[:]).then_inc(ln_step, 1)
                dve.wait_ge(ln_step, i * 2 + 2)
                dve.tensor_scalar(var, mv[:, :, 1], EPS, None, ALU.add).then_inc(var_ready, 1)
                post_norm(nc, dve, var, r0, t1, t2, rstd, ln_chain, i * 5, root, root_ready, i + 1)
                after(dve, x1_stored[p], it * 16, least)
                dve.tensor_scalar(x1_t[:, p, :], r_t[:], mv[:, 0, 0:1], rstd, ALU.subtract, ALU.mult
                                  ).then_inc(x1_ready, 1)

        for_pairs(dve, pair, before_last)

    def tensor(pe, before_last):
        pe.wait_ge(ones_ready, 1)
        pe.wait_ge(sums_ready, 1)
        nc.tensor.matmul(sum_ps, ones[:], sums[:], start=True, stop=True).then_inc(total_ready, 1)

        def pair(it, least, before_last=None):
            for p in range(2):
                if p == 1 and before_last:
                    before_last()
                i = it * 2 + p
                pe.wait_ge(z_lo_ready, i + 1)
                after(pe, r_ready, i - 1, 2 * least + p - 1)
                for h in range(H):
                    if isinstance(it, int) and i == 0 and h % HP == 0:
                        pe.wait_ge(wo_lo_ready, h // HP + 1)
                    a_hi, a_lo = zt_hi[p][:, h, :], zt_lo[p][:, h, :]
                    nc.tensor.matmul(out_ps[p][:], a_hi, wo_hi[:, h, :], start=(h == 0), stop=False)
                    nc.tensor.matmul(out_ps[p][:], a_hi, wo_lo[:, h, :], start=False, stop=False)
                    last = nc.tensor.matmul(out_ps[p][:], a_lo, wo_hi[:, h, :], start=False, stop=(h == H - 1))
                last.then_inc(out_full, 1)

        for_pairs(pe, pair, before_last)

    return dict(
        sync=sync, gpsimd=gpsimd, scalar=scalar, vector=vector, tensor=tensor, first_loads=first_loads,
        x1_stored=x1_stored, tiles=TILES, pairs=PAIRS, out_full=out_full, r_ready=r_ready, ternary=ternary)


def ffn_stage(nc, sem, sbuf, banks, ident, b2_all, before, T, DM, F, w1_t, w2_t, b1T, b2, x1_dram, out):
    C = DM // P
    FT = F // P
    LAG = 3
    HRING = 4
    sb = sbuf.put

    x1 = sb("w", "x1", [P, GROUPS, DM])
    x1b = sb("x", "x1b", [P, GROUPS, DM])
    b1_all = sb("own", "b1_all", [P, FT])
    xt_hi = sb("even", "xt_hi", [P, C, BANK], F32R)
    xt_lo = sb("even", "xt_lo", [P, C, BANK], F32R)
    g_t = sb("x", "g_t", [P, 2, BANK])
    h_hi = sb("x", "h_hi", [P, HRING, BANK], F32R)
    h_lo = sb("x", "h_lo", [P, HRING, BANK], F32R)
    r_t = sb("x", "r_t3", [P, GROUPS, DM])
    y_t = sb("x", "y_t", [P, GROUPS, DM])
    st = sb("own", "st3", [P, GROUPS, nc.vector.BN_STATS_DIM])
    mv = sb("own", "mv3", [P, GROUPS, nc.vector.BN_AGGR_DIM])
    small = sb("own", "small3", [P, 7, GROUPS])
    var, root, r0, t1, t2, rstd = (small[:, n, :] for n in range(6))
    acc, up = banks[0:3] + banks[6:7], banks[4:6]
    tp = [banks[3], banks[7]] + up

    bias_loaded = sem("bias_loaded")
    x1_loaded = sem("x1_loaded")
    x1b_ready = sem("x1b_ready")
    t_full = sem("t_full")
    t_hi = sem("t_hi")
    t_lo = sem("t_lo")
    up_full = sem("up_full")
    gelu_done = sem("gelu_done")
    h_hi_ready = sem("h_hi_ready")
    h_lo_ready = sem("h_lo_ready")
    acc_full = sem("acc_full")
    r_ready = sem("r_ready3")
    stats_ready = sem("stats_ready")
    aggr_ready = sem("aggr_ready")
    ln_chain = sem("ln_chain3")
    var_ready = sem("var_ready3")
    root_ready = sem("root_ready3")
    y_ready = sem("y_ready")
    y_stored = sem("y_stored")

    x1_v = x1_dram.rearrange("(g i p) d -> g p i d", p=P, i=GROUPS)
    out_v = out.rearrange("(g i p) d -> g p i d", p=P, i=GROUPS)

    def after(eng, s, value, least):
        if least > 0:
            eng.wait_ge(s, value)

    def for_groups(eng, group):
        group(0, 0)
        with eng.Fori(1, GROUPS - 1) as g:
            group(g, 1)
        group(GROUPS - 1, GROUPS - 1)


    def load_first(sp):
        for s in before["x1_stored"]:
            sp.wait_ge(s, 16 * GROUPS // 2)
        sp.dma_start(x1[:], x1_v[0, :, :, :]).then_inc(x1_loaded, 16)

    def sync(sp):
        sp.dma_start(b1_all[:], b1T[:, :]).then_inc(bias_loaded, 16)
        sp.dma_start(b2_all[:], b2.rearrange("(a d) -> a d", a=1).to_broadcast([P, DM])
                     ).then_inc(bias_loaded, 16)

        for s in before["x1_stored"]:
            sp.wait_ge(s, 16 * before["pairs"])

        def group(g, least):
            if not (isinstance(g, int) and g == GROUPS - 1):
                sp.wait_ge(t_lo, g * C + C)
                sp.wait_ge(x1b_ready, g * GROUPS + GROUPS)
                sp.dma_start(x1[:], x1_v[g + 1, :, :, :]).then_inc(x1_loaded, 16)
            for i in range(GROUPS):
                sp.wait_ge(y_ready, g * GROUPS + (i + 1))
                sp.dma_start(out_v[g, :, i, :], y_t[:, i, :]).then_inc(y_stored, 16)

        for_groups(sp, group)
        sp.wait_ge(y_stored, 16 * GROUPS * GROUPS)

    def gpsimd(pool):
        pool.wait_ge(before["out_full"], before["tiles"])
        pool.wait_ge(bias_loaded, 32)

        def group(g, least):
            pool.wait_ge(x1_loaded, g * 16 + 16)
            after(pool, r_ready, g * GROUPS, least)
            for i in range(GROUPS):
                last = pool.tensor_tensor(x1b[:, i, :], x1[:, i, :], b2_all[:], ALU.add)
                last.then_inc(x1b_ready, 1)

        for_groups(pool, group)

    def transposed_hi(act, g):
        for c in range(C):
            act.wait_ge(t_full, g * C + (c + 1))
            nc.scalar.activation(xt_hi[:, c, :], tp[c][:], ACT.Copy).then_inc(t_hi, 1)

    def scalar(act):
        act.wait_ge(bias_loaded, 32)

        def root_of(turn, least):
            if least > 0:
                act.wait_ge(var_ready, turn)
                nc.scalar.activation(root, var, ACT.Sqrt).then_inc(root_ready, 1)

        def group(g, least):
            for f in range(FT):
                if f == LAG:
                    root_of(g, least)
                act.wait_ge(up_full, g * FT + (f + 1))
                after(act, h_lo_ready, g * FT + (f - 1), least * FT + f - 1)
                nc.scalar.activation(g_t[:, f % 2, :], up[f % 2][:], ACT.Gelu, bias=b1_all[:, f:f + 1]
                                     ).then_inc(gelu_done, 1)
            if not (isinstance(g, int) and g == GROUPS - 1):
                transposed_hi(act, g + 1)
        for_groups(act, group)
        root_of(GROUPS, GROUPS)

    def transposed_lo(dve, g):
        for c in range(C):
            dve.wait_ge(t_hi, g * C + (c + 1))
            dve.tensor_tensor(xt_lo[:, c, :], tp[c][:], xt_hi[:, c, :].bitcast(F32), ALU.subtract
                              ).then_inc(t_lo, 1)

    def vector(dve):

        def finish(turn, least):
            if least > 0:
                post_norm(nc, dve, var, r0, t1, t2, rstd, ln_chain, turn * 5 - 5, root, root_ready, turn)
                for i in range(GROUPS):
                    dve.tensor_scalar(y_t[:, i, :], r_t[:, i, :], mv[:, i, 0:1], rstd[:, i:i + 1], ALU.subtract,
                                      ALU.mult).then_inc(y_ready, 1)

        def group(g, least):
            for f in range(FT):
                if f == LAG:
                    finish(g, least)
                dve.wait_ge(gelu_done, g * FT + (f + 1))
                dve.tensor_copy(h_hi[:, f % HRING, :], g_t[:, f % 2, :]).then_inc(h_hi_ready, 1)
                dve.wait_ge(h_hi_ready, g * FT + (f + 1))
                dve.tensor_tensor(h_lo[:, f % HRING, :], g_t[:, f % 2, :],
                                  h_hi[:, f % HRING, :].bitcast(F32), ALU.subtract).then_inc(h_lo_ready, 1)
            if not (isinstance(g, int) and g == GROUPS - 1):
                transposed_lo(dve, g + 1)
            dve.wait_ge(x1b_ready, g * GROUPS + GROUPS)
            after(dve, y_ready, g * GROUPS, least)
            after(dve, y_stored, g * 16 * GROUPS, least)
            for i in range(GROUPS):
                dve.wait_ge(acc_full, g * GROUPS + (i + 1))
                dve.tensor_tensor(r_t[:, i, :], acc[i][:], x1b[:, i, :], ALU.add).then_inc(r_ready, 1)
                dve.wait_ge(r_ready, g * GROUPS + (i + 1))
                dve.bn_stats(st[:, i, :], r_t[:, i, :]).then_inc(stats_ready, 1)
            dve.wait_ge(stats_ready, g * GROUPS + GROUPS)
            dve.memset(small[:, 6, :], 0.0)
            for i in range(GROUPS):
                dve.bn_aggr(mv[:, i, :], st[:, i, :]).then_inc(aggr_ready, 1)
            dve.wait_ge(aggr_ready, g * GROUPS + GROUPS)
            dve.tensor_scalar(var, mv[:, :, 1], EPS, None, ALU.add).then_inc(var_ready, 1)

        for_groups(dve, group)
        finish(GROUPS, GROUPS)

    def transpose_group(pe, g, least):
        pe.wait_ge(x1_loaded, g * 16 + 16)
        for c in range(C):
            if c >= 2:
                after(pe, gelu_done, g * FT + (c - 3), (least - 1) * FT + 1)
            for i in range(GROUPS):
                last = nc.tensor.transpose(tp[c][:, i * P:(i + 1) * P],
                                           x1[:, i, c * P:(c + 1) * P], ident[:])
            last.then_inc(t_full, 1)

    def tensor(pe):
        def first_product(g, f, least):
            after(pe, gelu_done, g * FT + (f - 1), least * FT + f - 1)
            for c in range(C):
                w = w1_t[:, c, f * P:(f + 1) * P]
                nc.tensor.matmul(up[f % 2][:], w, xt_hi[:, c, :], start=(c == 0), stop=False)
                last = nc.tensor.matmul(up[f % 2][:], w, xt_lo[:, c, :], start=False, stop=(c == C - 1))
            last.then_inc(up_full, 1)

        def second_product(g, f, least):
            pe.wait_ge(h_lo_ready, g * FT + (f + 1))
            for i in range(GROUPS):
                if isinstance(g, int) and g == 0 and f == 0 and i == 0:
                    pe.wait_ge(before["ternary"], before["tiles"])
                    pe.wait_ge(before["r_ready"], before["tiles"])
                if f == 0:
                    after(pe, r_ready, g * GROUPS + (i + 1 - GROUPS), (least - 1) * GROUPS + i + 1)
                tok = slice(i * P, (i + 1) * P)
                nc.tensor.matmul(acc[i][:], h_hi[:, f % HRING, tok], w2_t[:, f, :], start=(f == 0), stop=False)
                last = nc.tensor.matmul(acc[i][:], h_lo[:, f % HRING, tok], w2_t[:, f, :], start=False,
                                        stop=(f == FT - 1))
                if f == FT - 1:
                    last.then_inc(acc_full, 1)

        def group(g, least):
            if isinstance(g, int) and g == 0:
                pe.wait_ge(before["ternary"], before["tiles"] - 1)
            pe.wait_ge(t_lo, g * C + C)
            for f in range(FT):
                first_product(g, f, least)
                if f >= LAG:
                    second_product(g, f - LAG, least)
            if not (isinstance(g, int) and g == GROUPS - 1):
                transpose_group(pe, g + 1, least + 1)
            for f in range(FT - LAG, FT):
                second_product(g, f, least)

        for_groups(pe, group)

    return dict(
        sync=sync, gpsimd=gpsimd, scalar=scalar, vector=vector, tensor=tensor, load_first=load_first,
        transpose_group=transpose_group, transposed_hi=transposed_hi, transposed_lo=transposed_lo)


def layer(nc, a, out):
    T, DM = a["x"].shape
    H, _, DH = a["wq"].shape
    F = a["b1T"].shape[0] * a["b1T"].shape[1]
    z_dram = nc.dram_tensor("z_scratch", (GROUPS, GROUPS, DH, H, P), F32, kind="Internal").ap()
    x1_dram = nc.dram_tensor("x1_scratch", (T, DM), F32, kind="Internal").ap()
    with ExitStack() as ctx:
        def sem(name):
            return ctx.enter_context(nc.semaphore(name))

        banks = [ctx.enter_context(nc.psum_tensor(f"bank{n}", [P, BANK], F32)) for n in range(8)]
        sbuf = Map(nc)
        ident = sbuf.put("own", "ident", [P, P])
        abs_sums = sbuf.put("own", "abs_sums", [P, 2, H])
        attention = attention_stage(nc, sem, sbuf, banks, ident, H, T, DM, DH, a["xT"], a["wq"], a["wk"], a["wv"],
                                    a["bqkv"], a["w1"], a["w2T"], abs_sums, z_dram)
        sbuf.stage()
        w1_t = sbuf.put("v", "w1_t", [P, DM // P, F], F32R)
        w2_t = sbuf.put("v", "w2_t", [P, F // P, DM], F32R)
        projection = projection_stage(nc, sem, sbuf, banks, attention, H, T, DM, F, a["x"], a["wo"], a["bo"],
                                      a["w1T"], a["w2T"], abs_sums, w1_t, w2_t, z_dram, x1_dram)
        b2_all = sbuf.put("q", "b2_all", [P, DM])
        sbuf.stage()
        ffn = ffn_stage(nc, sem, sbuf, banks, ident, b2_all, projection, T, DM, F, w1_t, w2_t, a["b1T"], a["b2"], x1_dram,
                        out)

        with nc.Block() as block:

            @block.sync
            def _(sp):
                attention["sync"](sp, projection["first_loads"])
                projection["sync"](sp, lambda: ffn["load_first"](sp))
                ffn["sync"](sp)

            @block.gpsimd
            def _(pool):
                attention["gpsimd"](pool)
                projection["gpsimd"](pool)
                ffn["gpsimd"](pool)

            @block.scalar
            def _(act):
                attention["scalar"](act)
                projection["scalar"](act, lambda: ffn["transposed_hi"](act, 0))
                ffn["scalar"](act)

            @block.vector
            def _(dve):
                attention["vector"](dve)
                projection["vector"](dve, lambda: ffn["transposed_lo"](dve, 0))
                ffn["vector"](dve)

            @block.tensor
            def _(pe):
                attention["tensor"](pe)
                projection["tensor"](pe, lambda: ffn["transpose_group"](pe, 0, 0))
                ffn["tensor"](pe)


def kernel(**inputs):
    import numpy as np
    import concourse.bacc as bacc
    from concourse.bass_utils import run_bass_kernel_spmd

    def get(name):
        return np.asarray(inputs["L0_" + name])

    x = get("attn_x")[0]
    w1, w2 = get("ffn_w1"), get("ffn_w2")
    F, DM = w1.shape
    arrays = {
        "x": x, "xT": x.T,
        "wq": get("attn_W_Q"), "wk": get("attn_W_K"), "wv": get("attn_W_V"), "wo": get("attn_W_O"),
        "bqkv": np.stack([get("attn_b_Q"), get("attn_b_K"), get("attn_b_V")], axis=-1), "bo": get("attn_b_O"),
        "w1": w1, "w1T": w1.T.reshape(DM // P, P, 2, F // 2).transpose(0, 2, 1, 3).reshape(-1, P, F // 2),
        "w2T": w2.T, "b1T": get("ffn_b1").reshape(F // P, P).T, "b2": get("ffn_b2"),
    }
    arrays = {n: np.ascontiguousarray(v) for n, v in arrays.items()}
    nc = bacc.Bacc("TRN2", target_bir_lowering=False, num_devices=1)
    aps = {n: nc.dram_tensor("in_" + n, v.shape, mybir.dt.from_np(v.dtype), kind="ExternalInput").ap()
           for n, v in arrays.items()}
    out = nc.dram_tensor("out", x.shape, F32, kind="ExternalOutput").ap()
    layer(nc, aps, out)
    r = run_bass_kernel_spmd(nc, [{"in_" + n: v for n, v in arrays.items()}], core_ids=[0])
    return r.results[0]["out"].reshape(1, *x.shape)
```

```python
from contextlib import ExitStack

import concourse.bass as bass
from concourse import mybir

F32 = mybir.dt.float32
F32R = mybir.dt.float32r
BF16 = mybir.dt.bfloat16
ALU = mybir.AluOpType
ACT = mybir.ActivationFunctionType
AX_X = mybir.AxisListType.X

P = 128
BANK = 512
EPS = 1e-5
MASKED = -1.0e5

GROUPS = 4
RING = 3
SRING = 4
PTRING = 4
EVENTS = GROUPS * sum(n + 1 for n in range(GROUPS))
KTS = EVENTS
HI_UNITS = KTS + 4 * GROUPS
UNITS = HI_UNITS + GROUPS
CARRY_K = GROUPS * GROUPS
CARRY_U = CARRY_K + 1


def event(g, j, b):
    return sum(4 * (n + 1) for n in range(g)) + j * (g + 1) + b


def head_order(first):
    items, u, m = [], 0, 0
    for g in range(GROUPS):
        gp = (g - 1) % GROUPS
        carried = -EVENTS if g == 0 else 0
        prev = not (first and g == 0)
        tail = [("exp", gp, 3, b, event(gp, 3, b) + carried) for b in range(gp + 1)] if prev else []
        items += tail[:2]
        items.append(("q", g, u)); u += 1
        items += tail[2:3]
        items.append(("k", g, u)); u += 1
        pend = []
        if prev:
            items.append(("kt", gp, 0, u, m, carried)); pend.append((0, u, m)); u += 1; m += 1
        items += tail[3:]
        items.append(("vt", g, u)); u += 1
        if prev:
            items.append(("sum", gp, carried))
        for j in range(GROUPS):
            kts = [j * (gp + 1) + n for n in range(gp + 1)] if prev else []
            if j == 0:
                kts = kts[1:]
            exps = [("exp", g, j - 1, b, event(g, j - 1, b)) for b in range(g + 1)] if j else []
            for b in range(g + 1):
                for _ in range(min(len(kts), 2 if b == 0 else 1)):
                    kt = kts.pop(0)
                    items.append(("kt", gp, kt, u, m, carried)); pend.append((kt, u, m)); u += 1; m += 1
                    items += exps[:1]; del exps[:1]
                    if len(pend) > 2:
                        items.append(("pv", gp) + pend.pop(0))
                while exps and exps[0][4] <= event(g, j, b) - SRING:
                    items.append(exps.pop(0))
                items.append(("s", g, j, b, event(g, j, b)))
            for kt in kts:
                items.append(("kt", gp, kt, u, m, carried)); pend.append((kt, u, m)); u += 1; m += 1
                items += exps[:1]; del exps[:1]
                if len(pend) > 2:
                    items.append(("pv", gp) + pend.pop(0))
            items += exps
            if g == (1 if first else 0) and j in (1, 2):
                items.append(("ffn_sum", j - 1))
        items.append(("v", g, u)); u += 1
        items += [("pv", gp) + x for x in pend]
        if prev:
            items.append(("norm", gp, u, g)); u += 1
    return items


def tail_order():
    gp, items, pend = GROUPS - 1, [], []
    items += [("exp", gp, 3, b, event(gp, 3, b) - EVENTS) for b in range(gp + 1)]
    items.append(("sum", gp, -EVENTS))
    for kt in range(4 * (gp + 1)):
        items.append(("kt", gp, kt, kt, kt, -EVENTS)); pend.append((kt, kt, kt))
        if kt == 4 * gp + 3:
            items.append(("fill", gp))
        if len(pend) > 2:
            items.append(("pv", gp) + pend.pop(0))
    items += [("pv", gp) + x for x in pend]
    items.append(("norm", gp, 4 * (gp + 1), 0))
    return items


def hi_index(order):
    units = [it[3] if it[0] == "kt" else it[2] for it in order if it[0] in ("q", "k", "vt", "v", "kt")]
    return {u: n for n, u in enumerate(units)}


class Map:
    ZONES = {"x": 64, "w": 18, "even": 24, "k": 16, "v": 16, "odd": 32, "pt": 16, "q": 16, "own": 5}

    def __init__(self, nc):
        self.nc, self.next = nc, {}
        at = -(-nc.sbuf_base // 64) * 64
        for zone, kib in self.ZONES.items():
            self.next[zone] = at
            at += kib * 1024
        self.start = dict(self.next)
        assert at <= nc.sbuf_usable_end

    def stage(self):
        self.next = {z: self.next[z] if z == "own" else a for z, a in self.start.items()}

    def put(self, zone, name, shape, dt=F32):
        size = 2 if dt == BF16 else 4
        for n in shape[1:]:
            size *= n
        t = self.nc.alloc_sbuf_tensor_at(name, shape, dt, offset=self.next[zone])
        self.next[zone] += -(-size // 32) * 32
        return t


def attention_stage(nc, sem, sbuf, banks, ident, H, T, DM, DH, xT, wq, wk, wv, bqkv, f1, f2, abs_sums, z_dram,
                    rinv_dram):
    C = DM // P
    SCALE = float(DH) ** -0.5
    NEG = MASKED / SCALE
    assert DH == P and T == GROUPS * BANK and C == 4
    sb = sbuf.put

    x_hi = sb("x", "x_hi", [P, C, T], F32R)
    x_lo = sb("x", "x_lo", [P, C, T], F32R)
    k_hi = sb("k", "k_hi", [P, T], F32R)
    k_lo = sb("k", "k_lo", [P, T], F32R)
    v_hi = sb("v", "v_hi", [P, T], F32R)
    v_lo = sb("v", "v_lo", [P, T], F32R)
    q_hi = sb("q", "q_hi", [P, BANK], F32R)
    q_lo = sb("q", "q_lo", [P, BANK], F32R)
    vt = sb("q", "vt", [P, BANK])
    probs_even = sb("even", "probs_even", [P, GROUPS, 3 * BANK])
    probs_odd = sb("odd", "probs_odd", [P, GROUPS, 4 * BANK])
    pt_hi = sb("pt", "pt_hi", [P, PTRING, BANK], F32R)
    pt_lo = sb("pt", "pt_lo", [P, PTRING, BANK], F32R)
    rinv_all = sb("q", "rinv_all", [P, BANK])
    z_out = sb("q", "z_out", [P, 2, BANK])
    w_raw = sb("w", "w_raw", [P, 3, C, DH])
    w_hi = sb("w", "w_hi", [P, 3, C, DH], F32R)
    w_lo = sb("w", "w_lo", [P, 3, C, DH], F32R)
    b_raw = sb("own", "b_raw", [P, 4])
    b_cur = sb("own", "b_cur", [P, 4])
    zeros = sb("own", "zeros", [P, 4])
    ident_bf = sb("own", "ident_bf", [P, P], BF16)
    mask_bf = sb("own", "mask_bf", [P, P], BF16)
    f_raw = sb("q", "f_raw", [P, 2, DM])
    mx = sb("own", "mx", [P, 2, GROUPS])
    mx_scaled = sb("own", "mx_scaled", [P, GROUPS])
    neg_max = sb("own", "neg_max", [P, 2, GROUPS])
    sums = sb("own", "sums", [P, 2, GROUPS, GROUPS])
    total = sb("own", "total", [P, GROUPS])
    rinv = sb("own", "rinv", [P, GROUPS])
    probs = [probs_even, probs_odd]

    score, ring, z_ps = banks[0:SRING], banks[SRING:SRING + RING], banks[SRING + RING]

    x_loaded = [sem(f"x_loaded{g}") for g in range(GROUPS)]
    x_hi_ready = sem("x_hi_ready")
    x_lo_ready = sem("x_lo_ready")
    first_q_loaded = sem("first_q_loaded")
    first_kv_loaded = sem("first_kv_loaded")
    first_q_split = sem("first_q_split")
    w_loaded = sem("w_loaded")
    w_part = sem("w_part")
    w_ready = sem("w_ready")
    consts = sem("consts")
    ring_full = sem("ring_full")
    ring_hi = sem("ring_hi")
    ring_lo = sem("ring_lo")
    score_full = sem("score_full")
    max_part = sem("max_part")
    max_ready = sem("max_ready")
    exp_done = sem("exp_done")
    sum_part = sem("sum_part")
    rinv_ready = sem("rinv_ready")
    rinv_saved = sem("rinv_saved")
    rinv_spread = sem("rinv_spread")
    z_stored = [sem(f"z_stored{n}") for n in range(2)]
    f_loaded = sem("f_loaded")
    f_summed = sem("f_summed")

    f1_v, f2_v = (f.rearrange("(n p) d -> n p d", p=P) for f in (f1, f2))
    assert f1_v.shape[0] == f2_v.shape[0] == H

    def load_weights(eng, h, q_loaded, kv_loaded):
        eng.dma_start(w_raw[:, 0, :, :], wq[h, :, :].rearrange("(c p) e -> p c e", p=P)).then_inc(q_loaded, 16)
        eng.dma_start(b_raw[:, 0:3], bqkv[h, :, :]).then_inc(q_loaded, 16)
        for n, w in ((1, wk), (2, wv)):
            eng.dma_start(w_raw[:, n, :, :], w[h, :, :].rearrange("(c p) e -> p c e", p=P)
                          ).then_inc(kv_loaded, 16)

    def count(eng, s, per_head, h, n):
        if isinstance(h, int):
            if h * per_head + n > 0:
                eng.wait_ge(s, h * per_head + n)
        else:
            assert per_head + n > 0
            eng.wait_ge(s, h * per_head + n)

    def bank(first, u):
        return (u if first else u - CARRY_U) % RING

    def slot(first, m):
        return (m if first else m - CARRY_K) % PTRING

    def for_heads(eng, run):
        run(0, head_order(True), True)
        with eng.Fori(1, H) as h:
            run(h, head_order(False), False)
        run(H, tail_order(), False)

    LAST_VT = [it[2] for it in head_order(False) if it[0] == "vt"][-1] - CARRY_U
    last_vt = (H - 1) * UNITS + LAST_VT + 1

    def sync(sp, before_norm, before_tail):
        for g in range(GROUPS):
            blk = slice(g * BANK, (g + 1) * BANK)
            if g == 1:
                sp.wait_ge(first_kv_loaded, 32)
            sp.dma_start(probs_odd[:, :, blk], xT.rearrange("(c p) t -> p c t", p=P)[:, :, blk]
                         ).then_inc(x_loaded[g], 16)

        def load_ffn_slices(h):
            for n, f in enumerate((f1_v, f2_v)):
                count(sp, f_summed, 2, h, 0)
                sp.dma_start(f_raw[:, n, :], f[h, :, :]).then_inc(f_loaded, 16)

        def run(h, order, first):
            for it in order:
                if it[0] == "sum":
                    _, gp, carried = it
                    n = gp + 1 - (GROUPS if carried else 0)
                    count(sp, rinv_ready, GROUPS, h, n)
                    sp.dma_start(rinv_dram.rearrange("(p j) -> p j", p=P), rinv[:]).then_inc(rinv_saved, 16)
                    count(sp, rinv_saved, 16 * GROUPS, h, 16 * n)
                    sp.dma_start(rinv_all[:], rinv_dram.rearrange("(a q) -> a q", a=1).to_broadcast([P, BANK])
                                 ).then_inc(rinv_spread, 16)
                if it[0] == "norm":
                    _, gp, u, _ = it
                    hz = h - 1 if gp == GROUPS - 1 else h
                    count(sp, ring_lo, UNITS, h, u + 1 - (0 if first else CARRY_U))
                    slot_z = gp % 2
                    sp.dma_start(z_dram[gp, :, :, hz, :].rearrange("i e q -> e i q"),
                                 z_out[:, slot_z, :].rearrange("e (i q) -> e i q", q=P)
                                 ).then_inc(z_stored[slot_z], 16)

        def run_last(h, order, first):
            run(h, order[:-1], first)
            sp.wait_ge(ring_lo, last_vt)
            before_norm(sp)
            run(h, order[-1:], first)

        load_ffn_slices(0)
        run(0, head_order(True), True)
        with sp.Fori(1, H - 1) as h:
            load_ffn_slices(h)
            run(h, head_order(False), False)
        load_ffn_slices(H - 1)
        run_last(H - 1, head_order(False), False)
        run(H, tail_order()[:-1], False)
        before_tail(sp)
        run(H, tail_order()[-1:], False)

    def gpsimd(pool):
        pool.memset(ident[:], 0.0).then_inc(consts, 1)
        pool.memset(ident_bf[:], 0.0).then_inc(consts, 1)
        pool.memset(mask_bf[:], 0.0).then_inc(consts, 1)
        pool.memset(zeros[:], 0.0).then_inc(consts, 1)
        pool.wait_ge(consts, 4)
        for m in (ident, ident_bf):
            pool.affine_select(out=m[:], in_=m[:], compare_op=ALU.not_equal, fill=1.0, base=0,
                               pattern=[[-1, P]], channel_multiplier=1).then_inc(consts, 1)
        pool.affine_select(out=mask_bf[:], in_=mask_bf[:], compare_op=ALU.is_ge, fill=NEG, base=0,
                           pattern=[[-1, P]], channel_multiplier=1).then_inc(consts, 1)

        def split(h, first):
            if first:
                pool.wait_ge(first_q_loaded, 32)
            else:
                pool.wait_ge(w_loaded, h * 64)
            pool.tensor_tensor(b_cur[:, 0:3], b_raw[:, 0:3], zeros[:, 0:3], ALU.add).then_inc(w_part, 1)
            if first:
                pool.wait_ge(first_kv_loaded, 32)
            for n in range(1 if first else 0, 3):
                pool.tensor_scalar(w_hi[:, n, :, :], w_raw[:, n, :, :], 1.0, 0.0, ALU.mult, ALU.add
                                   ).then_inc(w_part, 1)
                if first:
                    pool.wait_ge(w_part, 2 * n)
                else:
                    pool.wait_ge(w_part, h * 6 + 2 * n)
                last = pool.tensor_tensor(w_lo[:, n, :, :], w_raw[:, n, :, :],
                                          w_hi[:, n, :, :].bitcast(F32), ALU.subtract)
                last.then_inc(w_part if n < 2 else w_ready, 1)

        split(0, True)
        pool.wait_ge(first_q_split, 2)
        with pool.Fori(1, H) as h:
            pool.wait_ge(w_part, h * 6 - 2)
            pool.wait_ge(w_ready, h)
            load_weights(pool, h, w_loaded, w_loaded)
            pool.wait_ge(ring_lo, (h - 1) * UNITS + (LAST_VT + 1))
            split(h, False)

    def scalar(act):
        def hi_part(out, src, bias=None):
            if bias is None:
                return nc.scalar.activation(out, src, ACT.Copy)
            return nc.scalar.activation(out, src, ACT.Identity, bias=bias)

        load_weights(act, 0, first_q_loaded, first_kv_loaded)

        def x_part(g, cs=slice(0, C)):
            blk = slice(g * BANK, (g + 1) * BANK)
            act.wait_ge(x_loaded[g], 16)
            hi_part(x_hi[:, cs, blk], probs_odd[:, cs, blk]).then_inc(x_hi_ready, 1)

        for c in (0, 2):
            x_part(0, slice(c, c + 2))
        x_part(1)

        def run(h, order, first):
            off = 0 if first else CARRY_U
            for it in order:
                kind, g = it[0], it[1]
                if kind in ("q", "k", "vt", "v"):
                    u = it[2]
                    src = ring[bank(first, u)]
                    count(act, ring_full, UNITS, h, u + 1 - off)
                    if kind == "q":
                        i = hi_part(q_hi[:], src[:], b_cur[:, 0:1])
                    elif kind == "k":
                        i = hi_part(k_hi[:, g * BANK:(g + 1) * BANK], src[:], b_cur[:, 1:2])
                    elif kind == "vt":
                        i = hi_part(vt[:, 0:BANK // 2], src[:, 0:BANK // 2], b_cur[:, 2:3])
                    else:
                        i = hi_part(v_hi[:, g * BANK:(g + 1) * BANK], src[:])
                    i.then_inc(ring_hi, 1)
                    if first and kind == "v" and g < 2:
                        x_part(g + 2)
                elif kind == "kt":
                    _, _, kt, u, m, _ = it
                    c0 = max(0, kt - 4 * g) * P
                    count(act, ring_full, UNITS, h, u + 1 - off)
                    hi_part(pt_hi[:, slot(first, m), c0:], ring[bank(first, u)][:, c0:]
                            ).then_inc(ring_hi, 1)
                elif kind == "exp":
                    _, _, j, b, e = it
                    w = P * (j + 1) if b == g else BANK
                    rows = GROUPS * g + j + 1 - (GROUPS * GROUPS if e < 0 else 0)
                    count(act, max_ready, GROUPS * GROUPS, h, rows)
                    nc.scalar.activation(probs[g % 2][:, j, b * BANK:b * BANK + w],
                                         score[e % SRING][:, 0:w], ACT.Exp,
                                         bias=neg_max[:, g % 2, j:j + 1], scale=SCALE,
                                         accum_out=sums[:, g % 2, j, b:b + 1]).then_inc(exp_done, 1)

        for_heads(act, run)

    def vector(dve):
        def x_part(g, cs=slice(0, C)):
            blk = slice(g * BANK, (g + 1) * BANK)
            dve.wait_ge(x_hi_ready, g + 2 if g else cs.start // 2 + 1)
            dve.tensor_tensor(x_lo[:, cs, blk], probs_odd[:, cs, blk], x_hi[:, cs, blk].bitcast(F32),
                              ALU.subtract).then_inc(x_lo_ready, 1)

        dve.wait_ge(first_q_loaded, 32)
        dve.tensor_copy(w_hi[:, 0, :, :], w_raw[:, 0, :, :]).then_inc(first_q_split, 1)
        dve.wait_ge(first_q_split, 1)
        dve.tensor_tensor(w_lo[:, 0, :, :], w_raw[:, 0, :, :], w_hi[:, 0, :, :].bitcast(F32), ALU.subtract
                          ).then_inc(first_q_split, 1)
        for c in (0, 2):
            x_part(0, slice(c, c + 2))
        x_part(1)

        def run(h, order, first):
            off = 0 if first else CARRY_U
            hi_off = 0 if first else CARRY_K
            hi = hi_index(order)
            for it in order:
                kind, g = it[0], it[1]
                if kind in ("q", "k", "vt", "v"):
                    u = it[2]
                    src = ring[bank(first, u)]
                    blk = slice(g * BANK, (g + 1) * BANK)
                    count(dve, ring_hi, HI_UNITS, h, hi[u] + 1 - hi_off)
                    if kind == "q":
                        i = dve.scalar_tensor_tensor(out=q_lo[:], in0=src[:], scalar=b_cur[:, 0:1],
                                                     in1=q_hi[:].bitcast(F32), op0=ALU.add,
                                                     op1=ALU.subtract)
                    elif kind == "k":
                        i = dve.scalar_tensor_tensor(out=k_lo[:, blk], in0=src[:], scalar=b_cur[:, 1:2],
                                                     in1=k_hi[:, blk].bitcast(F32), op0=ALU.add,
                                                     op1=ALU.subtract)
                    elif kind == "vt":
                        i = dve.tensor_scalar(vt[:, BANK // 2:], src[:, BANK // 2:], b_cur[:, 2:3], None,
                                              ALU.add)
                    else:
                        i = dve.tensor_tensor(v_lo[:, blk], src[:], v_hi[:, blk].bitcast(F32),
                                              ALU.subtract)
                    i.then_inc(ring_lo, 1)
                    if first and kind == "v" and g < 2:
                        x_part(g + 2)
                elif kind == "kt":
                    _, _, kt, u, m, _ = it
                    c0 = max(0, kt - 4 * g) * P
                    s = slot(first, m)
                    count(dve, ring_hi, HI_UNITS, h, hi[u] + 1 - hi_off)
                    dve.tensor_tensor(pt_lo[:, s, c0:], ring[bank(first, u)][:, c0:],
                                      pt_hi[:, s, c0:].bitcast(F32), ALU.subtract).then_inc(ring_lo, 1)
                elif kind == "norm":
                    _, gp, u, _ = it
                    stores = gp // 2 - (2 if gp == GROUPS - 1 else 0)
                    count(dve, z_stored[gp % 2], 16 * 2, h, 16 * stores)
                    count(dve, ring_full, UNITS, h, u + 1 - off)
                    count(dve, rinv_spread, 16 * GROUPS, h,
                          16 * (gp + 1 - (GROUPS if gp == GROUPS - 1 else 0)))
                    dve.tensor_tensor(z_out[:, gp % 2, :].rearrange("e (j p) -> e j p", p=P),
                                      z_ps[:].rearrange("e (j p) -> e j p", p=P),
                                      rinv_all[:].rearrange("e (p j) -> e j p", p=P), ALU.mult
                                      ).then_inc(ring_lo, 1)
                elif kind == "s":
                    _, _, j, b, e = it
                    w = P * (j + 1) if b == g else BANK
                    count(dve, score_full, EVENTS, h, e + 1)
                    dve.tensor_reduce(mx[:, j % 2, b:b + 1], score[e % SRING][:, 0:w], AX_X, ALU.max
                                      ).then_inc(max_part, 1)
                    if b == g:
                        count(dve, max_part, EVENTS, h, e + 1)
                        dve.tensor_scalar(mx_scaled[:, 0:g + 1], mx[:, j % 2, 0:g + 1], -SCALE, None,
                                          ALU.mult, ALU.min, accum_out=neg_max[:, g % 2, j:j + 1]
                                          ).then_inc(max_ready, 1)
                elif kind == "sum":
                    _, _, carried = it
                    n_sum = g + 1 - (GROUPS if carried else 0)
                    count(dve, exp_done, EVENTS, h, event(g, 3, g) + 1 + carried)
                    dve.tensor_reduce(total[:], sums[:, g % 2, :, 0:g + 1], AX_X, ALU.add
                                      ).then_inc(sum_part, 1)
                    count(dve, sum_part, GROUPS, h, n_sum)
                    dve.reciprocal(rinv[:], total[:]).then_inc(rinv_ready, 1)
                elif kind == "ffn_sum":
                    n = it[1]
                    dve.wait_ge(f_loaded, h * 32 + 32)
                    column = abs_sums[:, n, bass.ds(h, 1)] if not isinstance(h, int) \
                        else abs_sums[:, n, h:h + 1]
                    dve.tensor_reduce(column, f_raw[:, n, :], AX_X, ALU.add,
                                      apply_absolute_value=True).then_inc(f_summed, 1)

        for_heads(dve, run)

    def tensor(pe, fill):
        pe.wait_ge(consts, 7)

        def project(out, n, g, in_halves):
            blk = slice(g * BANK, (g + 1) * BANK)
            for c in range(C):
                if in_halves and c == 2:
                    pe.wait_ge(x_lo_ready, 2)
                nc.tensor.matmul(out, w_hi[:, n, c, :], x_hi[:, c, blk], start=(c == 0), stop=False)
                nc.tensor.matmul(out, w_hi[:, n, c, :], x_lo[:, c, blk], start=False, stop=False)
                last = nc.tensor.matmul(out, w_lo[:, n, c, :], x_hi[:, c, blk], start=False,
                                        stop=(c == C - 1))
            return last

        def run(h, order, first):
            off = 0 if first else CARRY_U
            for it in order:
                kind, g = it[0], it[1]
                if kind in ("q", "k", "vt", "v"):
                    u = it[2]
                    out = ring[bank(first, u)]
                    if first and g == 0 and kind != "vt" and kind != "v":
                        pe.wait_ge(w_part, 1 if kind == "q" else 3)
                    if first and g == 0 and kind == "q":
                        pe.wait_ge(first_q_split, 2)
                    if kind == ("vt" if first else "q") and g == 0:
                        pe.wait_ge(w_ready, h + 1)
                    if kind == "q" and first:
                        pe.wait_ge(x_lo_ready, g + 2 if g else 1)
                    count(pe, ring_lo, UNITS, h, u - RING + 1 - off)
                    if kind == "v":
                        u_vt = [x[2] for x in order if x[0] == "vt" and x[1] == g][0]
                        count(pe, ring_lo, UNITS, h, u_vt + 1 - off)
                        for t in range(GROUPS):
                            last = nc.tensor.transpose(out[:, t * P:(t + 1) * P],
                                                       vt[:, t * P:(t + 1) * P], ident[:])
                    else:
                        last = project(out[:], ("q", "k", "vt").index(kind), g, first and g == 0 and kind == "q")
                    last.then_inc(ring_full, 1)
                elif kind == "kt":
                    _, _, kt, u, m, carried = it
                    count(pe, ring_lo, UNITS, h, u - RING + 1 - off)
                    count(pe, exp_done, EVENTS, h, event(g, 3, kt // 4) + 1 + carried)
                    for j in range(max(0, kt - 4 * g), GROUPS):
                        last = nc.tensor.transpose(ring[bank(first, u)][:, j * P:(j + 1) * P],
                                                   probs[g % 2][:, j, kt * P:(kt + 1) * P], ident[:])
                    last.then_inc(ring_full, 1)
                elif kind == "fill":
                    fill(pe)
                elif kind == "pv":
                    _, _, kt, u, m = it
                    c0 = max(0, kt - 4 * g) * P
                    s = slot(first, m)
                    vs = slice(kt * P, (kt + 1) * P)
                    end = kt == 4 * g + 3
                    count(pe, ring_lo, UNITS, h, u + 1 - off)
                    nc.tensor.matmul(z_ps[:, c0:], v_hi[:, vs], pt_hi[:, s, c0:], start=(kt == 0), stop=False)
                    nc.tensor.matmul(z_ps[:, c0:], v_hi[:, vs], pt_lo[:, s, c0:], start=False, stop=False)
                    last = nc.tensor.matmul(z_ps[:, c0:], v_lo[:, vs], pt_hi[:, s, c0:], start=False, stop=end)
                    if end:
                        last.then_inc(ring_full, 1)
                elif kind == "s":
                    _, _, j, b, e = it
                    w = P * (j + 1) if b == g else BANK
                    keys = slice(b * BANK, b * BANK + w)
                    out = score[e % SRING][:, 0:w]
                    qs = slice(j * P, (j + 1) * P)
                    if j == 0 and b == 0:
                        u = [x[2] for x in order if x[0] == "k" and x[1] == g][0]
                        count(pe, ring_lo, UNITS, h, u + 1 - off)
                    count(pe, exp_done, EVENTS, h, e - SRING + 1)
                    nc.tensor.matmul(out, q_hi[:, qs], k_hi[:, keys], start=True, stop=False)
                    nc.tensor.matmul(out, q_hi[:, qs], k_lo[:, keys], start=False, stop=False)
                    last = nc.tensor.matmul(out, q_lo[:, qs], k_hi[:, keys], start=False, stop=(b < g))
                    if b == g:
                        last = nc.tensor.matmul(out[:, w - P:w], ident_bf[:], mask_bf[:], start=False,
                                                stop=True)
                    last.then_inc(score_full, 1)

        for_heads(pe, run)

    return dict(
        sync=sync, gpsimd=gpsimd, scalar=scalar, vector=vector, tensor=tensor, ring_lo=ring_lo,
        z_stored=z_stored, f_summed=f_summed,
        last_vt=last_vt, all_heads_units=UNITS * H - CARRY_U, stores=16 * GROUPS * H // 2,
        group_stored=lambda g: (z_stored[g % 2], 16 * (2 * (H - 1) + g // 2 + 1)))


def post_norm(nc, dve, var, r0, t1, t2, rstd, chain, base, root, root_ready, turn):
    dve.wait_ge(root_ready, turn)
    dve.reciprocal(r0, root).then_inc(chain, 1)
    dve.wait_ge(chain, base + 1)
    dve.tensor_tensor(t1, r0, r0, ALU.mult).then_inc(chain, 1)
    dve.wait_ge(chain, base + 2)
    dve.tensor_tensor(t2, t1, var, ALU.mult).then_inc(chain, 1)
    dve.wait_ge(chain, base + 3)
    dve.tensor_scalar(t1, t2, -0.5, 1.5, ALU.mult, ALU.add).then_inc(chain, 1)
    dve.wait_ge(chain, base + 4)
    dve.tensor_tensor(rstd, t1, r0, ALU.mult).then_inc(chain, 1)
    dve.wait_ge(chain, base + 5)


def projection_stage(nc, sem, sbuf, banks, before, H, T, DM, F, x, wo, bo, w1T, w2T, abs_sums, w1_t, w2_t, z_dram,
                     x1_dram):
    TILES = T // P
    PAIRS = TILES // 2
    HALF = F * (DM // P) // PAIRS
    WO_PARTS = 8
    HP = H // WO_PARTS
    FILL = H // 4
    sb = sbuf.put

    wo_hi = sb("x", "wo_hi", [P, H, DM], F32R)
    wo_lo = sb("x", "wo_lo", [P, H, DM], F32R)
    wo_raw = sb("w", "wo_raw", [P, 2, HP, DM])
    zt_raw = sb("w", "zt_raw", [P, H, P])
    zt_hi = [None, None]
    zt_lo = [None, None]
    zt_hi[0] = sb("even", "zt_hi0", [P, H, P], F32R)
    zt_lo[0] = sb("even", "zt_lo0", [P, H, P], F32R)
    zt_hi[1] = sb("even", "zt_hi1", [P, H, P], F32R)
    zt_lo[1] = sb("k", "zt_lo1", [P, H, P], F32R)
    x_t = sb("k", "x_t", [P, 2, DM])
    xb_t = sb("k", "xb_t", [P, 2, DM])
    bo_all = sb("w", "bo_all", [P, DM])
    r_t = sb("q", "r_t", [P, DM])
    x1_t = sb("q", "x1_t", [P, 2, DM])
    below = sb("q", "below", [P, HALF], BF16)
    b2_all = sb("q", "b2_all", [P, DM])
    sb("q", "spare", [P, DM])
    f_raw = sb("q", "f_raw2", [P, HALF])
    ones = sb("own", "ones", [P, P])
    sums = sb("own", "sums2", [P, 2])
    thr = sb("own", "thr", [P, 2])
    neg_thr = sb("own", "neg_thr", [P, 2])
    st = sb("own", "st", [P, nc.vector.BN_STATS_DIM])
    mv = sb("own", "mv", [P, 1, nc.vector.BN_AGGR_DIM])
    small = sb("own", "small", [P, 8])
    var, root, r0, t1, t2, rstd = (small[:, n:n + 1] for n in range(6))
    out_ps = banks[0:2]
    sum_ps = banks[2][:, 0:2]

    wo_loaded = [sem(f"wo_loaded{n}") for n in range(2)]
    wo_hi_ready = sem("wo_hi_ready")
    wo_lo_ready = sem("wo_lo_ready")
    z_loaded = sem("z_loaded")
    z_hi_ready = sem("z_hi_ready")
    z_lo_ready = sem("z_lo_ready")
    x_loaded = [sem(f"x_loaded_s{n}") for n in range(2)]
    bo_loaded = sem("bo_loaded")
    xb_ready = sem("xb_ready")
    out_full = sem("out_full")
    r_ready = sem("r_ready")
    ln_step = sem("ln_step")
    ln_chain = sem("ln_chain")
    var_ready = sem("var_ready")
    root_ready = sem("root_ready")
    x1_ready = sem("x1_ready")
    x1_stored = [sem(f"x1_stored{n}") for n in range(2)]
    f_loaded = sem("f_loaded2")
    below_ready = sem("below_ready")
    ternary = sem("ternary")
    ones_ready = sem("ones_ready")
    sums_ready = sem("sums_ready")
    total_ready = sem("total_ready")
    scale_ready = sem("scale_ready")
    thr_ready = sem("thr_ready")

    x_v = x.rearrange("(i p) d -> i p d", p=P)
    x1_v = x1_dram.rearrange("(i p) d -> i p d", p=P)
    wo_v = wo.rearrange("h e d -> e h d")
    w2_v = w2T.rearrange("(n a p) d -> n p a d", p=P, a=HALF // DM)
    w1_flat = w1_t[:].rearrange("p c f -> p (c f)")
    w2_flat = w2_t[:].rearrange("p c d -> p (c d)")

    def after(eng, s, value, least):
        if least > 0:
            eng.wait_ge(s, value)

    def for_pairs(eng, pair, before_last=None):
        pair(0, 0)
        with eng.Fori(1, PAIRS - 1) as it:
            pair(it, 1)
        pair(PAIRS - 1, PAIRS - 1, before_last)

    def load_z(sp, i, least):
        after(sp, z_lo_ready, i, least)
        sp.dma_start(zt_raw[:], z_dram.rearrange("g i e h q -> (g i) e h q")[i, :, :, :]
                     ).then_inc(z_loaded, 16)

    def first_loads(sp):
        for n in range(WO_PARTS):
            if n >= 2:
                sp.wait_ge(wo_lo_ready, n - 1)
            sp.dma_start(wo_raw[:, n % 2, :, :], wo_v[:, n * HP:(n + 1) * HP, :]
                         ).then_inc(wo_loaded[n % 2], 16)
            if n == 1:
                sp.wait_ge(*before["group_stored"](0))
                load_z(sp, 0, 0)

    def second_loads(sp):
        sp.dma_start(bo_all[:], bo.rearrange("(a d) -> a d", a=1).to_broadcast([P, DM])
                     ).then_inc(bo_loaded, 16)
        load_z(sp, 1, 1)

    def sync(sp, before_last):
        sp.wait_ge(before["ring_lo"], before["all_heads_units"])
        sp.wait_ge(before["f_summed"], 2 * H)

        def pair(it, least, before_last=None):
            for p in range(2):
                if p == 1 and before_last:
                    before_last()
                i = it * 2 + p
                if isinstance(it, int) and i == 1:
                    for s in before["z_stored"]:
                        sp.wait_ge(s, before["stores"])
                if not (isinstance(it, int) and i in (0, TILES - 1)):
                    load_z(sp, i + 1, 2 * least + p + 1)
                after(sp, xb_ready, i - 1, 2 * least + p - 1)
                sp.dma_start(x_t[:, p, :], x_v[i, :, :]).then_inc(x_loaded[p], 16)
                after(sp, ternary, i, 2 * least + p)
                if p == 0:
                    sp.dma_start(f_raw[:], w1T[it, :, :]).then_inc(f_loaded, 16)
                else:
                    sp.dma_start(f_raw[:].rearrange("p (a d) -> p a d", d=DM), w2_v[it, :, :, :]
                                 ).then_inc(f_loaded, 16)

        for_pairs(sp, pair, before_last)

    def gpsimd(pool):
        def split(hi, lo, raw, hi_ready, lo_ready, count):
            pool.tensor_scalar(hi, raw, 1.0, 0.0, ALU.mult, ALU.add).then_inc(hi_ready, 1)
            pool.wait_ge(hi_ready, count)
            pool.tensor_tensor(lo, raw, hi.bitcast(F32), ALU.subtract).then_inc(lo_ready, 1)

        pool.wait_ge(before["ring_lo"], before["last_vt"])
        for n in range(WO_PARTS):
            if n == WO_PARTS - 2:
                pool.wait_ge(before["ring_lo"], before["all_heads_units"])
                pool.wait_ge(z_loaded, 16)
                split(zt_hi[0][:], zt_lo[0][:], zt_raw[:], z_hi_ready, z_lo_ready, 1)
            pool.wait_ge(wo_loaded[n % 2], 16 * (n // 2 + 1))
            hs = slice(n * HP, (n + 1) * HP)
            split(wo_hi[:, hs, :], wo_lo[:, hs, :], wo_raw[:, n % 2, :, :], wo_hi_ready, wo_lo_ready, n + 1)
        pool.wait_ge(bo_loaded, 16)

        def pair(it, least, before_last=None):
            for p in range(2):
                i = it * 2 + p
                pool.wait_ge(x_loaded[p], it * 16 + 16)
                after(pool, r_ready, i - 1, 2 * least + p - 1)
                pool.tensor_tensor(xb_t[:, p, :], x_t[:, p, :], bo_all[:], ALU.add).then_inc(xb_ready, 1)
                pool.wait_ge(x1_ready, i + 1)
                pool.dma_start(x1_v[i, :, :], x1_t[:, p, :]).then_inc(x1_stored[p], 16)

        for_pairs(pool, pair)

    def root_of(act, i):
        act.wait_ge(var_ready, i + 1)
        nc.scalar.activation(root, var, ACT.Sqrt).then_inc(root_ready, 1)

    def scalar(act, before_last):
        def z_part(i, p):
            act.wait_ge(z_loaded, i * 16 + 16)
            nc.scalar.activation(zt_hi[p][:], zt_raw[:], ACT.Copy).then_inc(z_hi_ready, 1)

        def pair(it, least, before_last=None):
            for p in range(2):
                if p == 1 and before_last:
                    before_last()
                i = it * 2 + p
                if not (isinstance(it, int) and i == TILES - 1):
                    after(act, out_full, i, 2 * least + p)
                    z_part(i + 1, 1 - p)
                if not (isinstance(it, int) and i == TILES - 1):
                    root_of(act, i)

        for_pairs(act, pair, before_last)

    def finish(dve, it, p, least):
        i = it * 2 + p
        post_norm(nc, dve, var, r0, t1, t2, rstd, ln_chain, i * 5, root, root_ready, i + 1)
        after(dve, x1_stored[p], it * 16, least)
        dve.tensor_scalar(x1_t[:, p, :], r_t[:], mv[:, 0, 0:1], rstd, ALU.subtract, ALU.mult
                          ).then_inc(x1_ready, 1)

    def vector(dve, before_last):
        def z_part(i, p):
            dve.wait_ge(z_hi_ready, i + 1)
            dve.tensor_tensor(zt_lo[p][:], zt_raw[:], zt_hi[p][:].bitcast(F32), ALU.subtract
                              ).then_inc(z_lo_ready, 1)

        def thresholds():
            dve.wait_ge(total_ready, 1)
            dve.tensor_scalar(thr[:], sum_ps, 1.0 / (F * DM), 0.7, ALU.mult, ALU.mult).then_inc(scale_ready, 1)
            dve.wait_ge(scale_ready, 1)
            dve.tensor_scalar(neg_thr[:], thr[:], -1.0, None, ALU.mult).then_inc(thr_ready, 1)
            dve.wait_ge(thr_ready, 1)

        dve.memset(ones[:], 1.0).then_inc(ones_ready, 1)
        dve.tensor_reduce(sums[:], abs_sums[:], AX_X, ALU.add).then_inc(sums_ready, 1)

        def pair(it, least, before_last=None):
            for p in range(2):
                if p == 1 and before_last:
                    before_last()
                i = it * 2 + p
                if not (isinstance(it, int) and i == TILES - 1):
                    z_part(i + 1, 1 - p)
                if isinstance(it, int) and i == 0:
                    thresholds()
                dve.wait_ge(out_full, i + 1)
                dve.wait_ge(xb_ready, i + 1)
                after(dve, x1_ready, i, 2 * least + p)
                dve.tensor_tensor(r_t[:], out_ps[p][:], xb_t[:, p, :], ALU.add).then_inc(r_ready, 1)
                dve.wait_ge(r_ready, i + 1)
                dve.bn_stats(st[:], r_t[:]).then_inc(ln_step, 1)
                dve.wait_ge(f_loaded, i * 16 + 16)
                dve.tensor_scalar(below[:], f_raw[:], neg_thr[:, p:p + 1], None, ALU.is_le
                                  ).then_inc(below_ready, 1)
                dve.wait_ge(ln_step, i * 2 + 1)
                dve.wait_ge(below_ready, i + 1)
                flat = (w1_flat, w2_flat)[p]
                dve.scalar_tensor_tensor(out=flat[:, bass.ds(it * HALF, HALF)], in0=f_raw[:],
                                         scalar=thr[:, p:p + 1], in1=below[:], op0=ALU.is_ge,
                                         op1=ALU.subtract).then_inc(ternary, 1)
                dve.bn_aggr(mv[:, 0, :], st[:]).then_inc(ln_step, 1)
                dve.wait_ge(ln_step, i * 2 + 2)
                dve.tensor_scalar(var, mv[:, :, 1], EPS, None, ALU.add).then_inc(var_ready, 1)
                if not (isinstance(it, int) and i == TILES - 1):
                    finish(dve, it, p, least)

        for_pairs(dve, pair, before_last)

    def tile_heads(pe, it, p, heads):
        for h in heads:
            if isinstance(it, int) and it == 0 and p == 0 and h % HP == 0:
                pe.wait_ge(wo_lo_ready, h // HP + 1)
            if isinstance(it, int) and it == 0 and p == 0 and h == 0:
                pe.wait_ge(z_lo_ready, 1)
            a_hi, a_lo = zt_hi[p][:, h, :], zt_lo[p][:, h, :]
            nc.tensor.matmul(out_ps[p][:], a_hi, wo_hi[:, h, :], start=(h == 0), stop=False)
            nc.tensor.matmul(out_ps[p][:], a_hi, wo_lo[:, h, :], start=False, stop=False)
            last = nc.tensor.matmul(out_ps[p][:], a_lo, wo_hi[:, h, :], start=False, stop=(h == H - 1))
            if h == H - 1:
                last.then_inc(out_full, 1)

    def tensor(pe, before_last):
        def pair(it, least, before_last=None):
            for p in range(2):
                if p == 1 and before_last:
                    before_last()
                i = it * 2 + p
                if isinstance(it, int) and i == 0:
                    tile_heads(pe, it, p, range(FILL, H))
                    pe.wait_ge(ones_ready, 1)
                    pe.wait_ge(sums_ready, 1)
                    nc.tensor.matmul(sum_ps, ones[:], sums[:], start=True, stop=True).then_inc(total_ready, 1)
                else:
                    pe.wait_ge(z_lo_ready, i + 1)
                    after(pe, r_ready, i - 1, 2 * least + p - 1)
                    tile_heads(pe, it, p, range(H))

        for_pairs(pe, pair, before_last)

    return dict(
        last_root=lambda act: root_of(act, TILES - 1), last_finish=lambda dve: finish(dve, PAIRS - 1, 1, PAIRS - 1),
        first_heads=lambda pe: tile_heads(pe, 0, 0, range(FILL)), b2_all=b2_all,
        sync=sync, gpsimd=gpsimd, scalar=scalar, vector=vector, tensor=tensor,
        first_loads=first_loads, second_loads=second_loads,
        x1_stored=x1_stored, tiles=TILES, pairs=PAIRS, out_full=out_full, r_ready=r_ready, ternary=ternary)


def ffn_stage(nc, sem, sbuf, banks, ident, b2_all, before, T, DM, F, w1_t, w2_t, b1T, b2, x1_dram, out):
    C = DM // P
    FT = F // P
    LAG = 3
    HRING = 4
    sb = sbuf.put

    x1 = sb("w", "x1", [P, GROUPS, DM])
    x1b = sb("x", "x1b", [P, GROUPS, DM])
    b1_all = sb("own", "b1_all", [P, FT])
    xt_hi = sb("even", "xt_hi", [P, C, BANK], F32R)
    xt_lo = sb("even", "xt_lo", [P, C, BANK], F32R)
    g_t = sb("x", "g_t", [P, 2, BANK])
    h_hi = sb("x", "h_hi", [P, HRING, BANK], F32R)
    h_lo = sb("x", "h_lo", [P, HRING, BANK], F32R)
    r_t = sb("x", "r_t3", [P, GROUPS, DM])
    y_t = sb("x", "y_t", [P, GROUPS, DM])
    st = sb("own", "st3", [P, GROUPS, nc.vector.BN_STATS_DIM])
    mv = sb("own", "mv3", [P, GROUPS, nc.vector.BN_AGGR_DIM])
    small = sb("own", "small3", [P, 7, GROUPS])
    var, root, r0, t1, t2, rstd = (small[:, n, :] for n in range(6))
    acc, up = banks[0:3] + banks[6:7], banks[4:6]
    tp = [banks[3], banks[7]] + up

    bias_loaded = sem("bias_loaded")
    x1_loaded = sem("x1_loaded")
    x1b_ready = sem("x1b_ready")
    t_full = sem("t_full")
    t_hi = sem("t_hi")
    t_lo = sem("t_lo")
    up_full = sem("up_full")
    gelu_done = sem("gelu_done")
    h_hi_ready = sem("h_hi_ready")
    h_lo_ready = sem("h_lo_ready")
    acc_full = sem("acc_full")
    r_ready = sem("r_ready3")
    stats_ready = sem("stats_ready")
    aggr_ready = sem("aggr_ready")
    ln_chain = sem("ln_chain3")
    var_ready = sem("var_ready3")
    root_ready = sem("root_ready3")
    y_ready = sem("y_ready")
    y_stored = sem("y_stored")

    x1_v = x1_dram.rearrange("(g i p) d -> g p i d", p=P, i=GROUPS)
    out_v = out.rearrange("(g i p) d -> g p i d", p=P, i=GROUPS)

    def after(eng, s, value, least):
        if least > 0:
            eng.wait_ge(s, value)

    def for_groups(eng, group):
        group(0, 0)
        with eng.Fori(1, GROUPS - 1) as g:
            group(g, 1)
        group(GROUPS - 1, GROUPS - 1)

    def load_first(sp):
        for s in before["x1_stored"]:
            sp.wait_ge(s, 16 * GROUPS // 2)
        sp.dma_start(x1[:], x1_v[0, :, :, :]).then_inc(x1_loaded, 16)

    def sync(sp):
        sp.dma_start(b1_all[:], b1T[:, :]).then_inc(bias_loaded, 16)
        sp.dma_start(b2_all[:], b2.rearrange("(a d) -> a d", a=1).to_broadcast([P, DM])
                     ).then_inc(bias_loaded, 16)

        for s in before["x1_stored"]:
            sp.wait_ge(s, 16 * before["pairs"])

        def group(g, least):
            if not (isinstance(g, int) and g == GROUPS - 1):
                sp.wait_ge(t_lo, g * C + C)
                sp.wait_ge(x1b_ready, g * GROUPS + GROUPS)
                sp.dma_start(x1[:], x1_v[g + 1, :, :, :]).then_inc(x1_loaded, 16)
            for i in range(GROUPS):
                sp.wait_ge(y_ready, g * GROUPS + (i + 1))
                sp.dma_start(out_v[g, :, i, :], y_t[:, i, :]).then_inc(y_stored, 16)

        for_groups(sp, group)
        sp.wait_ge(y_stored, 16 * GROUPS * GROUPS)

    def gpsimd(pool):
        pool.wait_ge(before["out_full"], before["tiles"])
        pool.wait_ge(bias_loaded, 32)

        def group(g, least):
            pool.wait_ge(x1_loaded, g * 16 + 16)
            after(pool, r_ready, g * GROUPS, least)
            for i in range(GROUPS):
                last = pool.tensor_tensor(x1b[:, i, :], x1[:, i, :], b2_all[:], ALU.add)
                last.then_inc(x1b_ready, 1)

        for_groups(pool, group)

    def transposed_hi(act, g):
        for c in range(C):
            act.wait_ge(t_full, g * C + (c + 1))
            nc.scalar.activation(xt_hi[:, c, :], tp[c][:], ACT.Copy).then_inc(t_hi, 1)

    def scalar(act):
        act.wait_ge(bias_loaded, 32)

        def root_of(turn, least):
            if least > 0:
                act.wait_ge(var_ready, turn)
                nc.scalar.activation(root, var, ACT.Sqrt).then_inc(root_ready, 1)

        def group(g, least):
            for f in range(FT):
                if f == LAG:
                    if isinstance(g, int) and g == 0:
                        before["last_root"](act)
                    root_of(g, least)
                act.wait_ge(up_full, g * FT + (f + 1))
                after(act, h_lo_ready, g * FT + (f - 1), least * FT + f - 1)
                nc.scalar.activation(g_t[:, f % 2, :], up[f % 2][:], ACT.Gelu, bias=b1_all[:, f:f + 1]
                                     ).then_inc(gelu_done, 1)
            if not (isinstance(g, int) and g == GROUPS - 1):
                transposed_hi(act, g + 1)
        for_groups(act, group)
        root_of(GROUPS, GROUPS)

    def transposed_lo(dve, g):
        for c in range(C):
            dve.wait_ge(t_hi, g * C + (c + 1))
            dve.tensor_tensor(xt_lo[:, c, :], tp[c][:], xt_hi[:, c, :].bitcast(F32), ALU.subtract
                              ).then_inc(t_lo, 1)

    def vector(dve):

        def finish(turn, least):
            if least > 0:
                post_norm(nc, dve, var, r0, t1, t2, rstd, ln_chain, turn * 5 - 5, root, root_ready, turn)
                for i in range(GROUPS):
                    dve.tensor_scalar(y_t[:, i, :], r_t[:, i, :], mv[:, i, 0:1], rstd[:, i:i + 1], ALU.subtract,
                                      ALU.mult).then_inc(y_ready, 1)

        def group(g, least):
            for f in range(FT):
                if f == LAG:
                    if isinstance(g, int) and g == 0:
                        before["last_finish"](dve)
                    finish(g, least)
                dve.wait_ge(gelu_done, g * FT + (f + 1))
                dve.tensor_copy(h_hi[:, f % HRING, :], g_t[:, f % 2, :]).then_inc(h_hi_ready, 1)
                dve.wait_ge(h_hi_ready, g * FT + (f + 1))
                dve.tensor_tensor(h_lo[:, f % HRING, :], g_t[:, f % 2, :],
                                  h_hi[:, f % HRING, :].bitcast(F32), ALU.subtract).then_inc(h_lo_ready, 1)
            if not (isinstance(g, int) and g == GROUPS - 1):
                transposed_lo(dve, g + 1)
            dve.wait_ge(x1b_ready, g * GROUPS + GROUPS)
            after(dve, y_ready, g * GROUPS, least)
            after(dve, y_stored, g * 16 * GROUPS, least)
            for i in range(GROUPS):
                dve.wait_ge(acc_full, g * GROUPS + (i + 1))
                dve.tensor_tensor(r_t[:, i, :], acc[i][:], x1b[:, i, :], ALU.add).then_inc(r_ready, 1)
                dve.wait_ge(r_ready, g * GROUPS + (i + 1))
                dve.bn_stats(st[:, i, :], r_t[:, i, :]).then_inc(stats_ready, 1)
            dve.wait_ge(stats_ready, g * GROUPS + GROUPS)
            dve.memset(small[:, 6, :], 0.0)
            for i in range(GROUPS):
                dve.bn_aggr(mv[:, i, :], st[:, i, :]).then_inc(aggr_ready, 1)
            dve.wait_ge(aggr_ready, g * GROUPS + GROUPS)
            dve.tensor_scalar(var, mv[:, :, 1], EPS, None, ALU.add).then_inc(var_ready, 1)

        for_groups(dve, group)
        finish(GROUPS, GROUPS)

    def transpose_group(pe, g, least):
        pe.wait_ge(x1_loaded, g * 16 + 16)
        for c in range(C):
            if c >= 2:
                after(pe, gelu_done, g * FT + (c - 3), (least - 1) * FT + 1)
            for i in range(GROUPS):
                last = nc.tensor.transpose(tp[c][:, i * P:(i + 1) * P],
                                           x1[:, i, c * P:(c + 1) * P], ident[:])
            last.then_inc(t_full, 1)

    def tensor(pe):
        def first_product(g, f, least):
            after(pe, gelu_done, g * FT + (f - 1), least * FT + f - 1)
            for c in range(C):
                w = w1_t[:, c, f * P:(f + 1) * P]
                nc.tensor.matmul(up[f % 2][:], w, xt_hi[:, c, :], start=(c == 0), stop=False)
                last = nc.tensor.matmul(up[f % 2][:], w, xt_lo[:, c, :], start=False, stop=(c == C - 1))
            last.then_inc(up_full, 1)

        def second_product(g, f, least, tiles=range(GROUPS)):
            pe.wait_ge(h_lo_ready, g * FT + (f + 1))
            for i in tiles:
                if isinstance(g, int) and g == 0 and f == 0 and i == 0:
                    pe.wait_ge(before["ternary"], before["tiles"])
                    pe.wait_ge(before["r_ready"], before["tiles"])
                if f == 0:
                    after(pe, r_ready, g * GROUPS + (i + 1 - GROUPS), (least - 1) * GROUPS + i + 1)
                tok = slice(i * P, (i + 1) * P)
                nc.tensor.matmul(acc[i][:], h_hi[:, f % HRING, tok], w2_t[:, f, :], start=(f == 0), stop=False)
                last = nc.tensor.matmul(acc[i][:], h_lo[:, f % HRING, tok], w2_t[:, f, :], start=False,
                                        stop=(f == FT - 1))
                if f == FT - 1:
                    last.then_inc(acc_full, 1)

        def group(g, least):
            if isinstance(g, int) and g == 0:
                pe.wait_ge(before["ternary"], before["tiles"] - 1)
            pe.wait_ge(t_lo, g * C + C)
            for f in range(FT):
                first_product(g, f, least)
                if f >= LAG:
                    second_product(g, f - LAG, least)
            if not (isinstance(g, int) and g == GROUPS - 1):
                transpose_group(pe, g + 1, least + 1)
            if isinstance(g, int) and g == GROUPS - 1:
                for i, lags in ((0, (3, 2)), (1, (3, 2)), (0, (1,)), (1, (1,)), (2, (3, 2, 1)), (3, (3, 2, 1))):
                    for lag in lags:
                        second_product(g, FT - lag, least, (i,))
            else:
                for f in range(FT - LAG, FT):
                    second_product(g, f, least)

        for_groups(pe, group)

    return dict(
        sync=sync, gpsimd=gpsimd, scalar=scalar, vector=vector, tensor=tensor, load_first=load_first,
        transpose_group=transpose_group, transposed_hi=transposed_hi, transposed_lo=transposed_lo)


def layer(nc, a, out):
    T, DM = a["x"].shape
    H, _, DH = a["wq"].shape
    F = a["b1T"].shape[0] * a["b1T"].shape[1]
    z_dram = nc.dram_tensor("z_scratch", (GROUPS, GROUPS, DH, H, P), F32, kind="Internal").ap()
    rinv_dram = nc.dram_tensor("rinv_scratch", (BANK,), F32, kind="Internal").ap()
    x1_dram = nc.dram_tensor("x1_scratch", (T, DM), F32, kind="Internal").ap()
    with ExitStack() as ctx:
        def sem(name):
            return ctx.enter_context(nc.semaphore(name))

        banks = [ctx.enter_context(nc.psum_tensor(f"bank{n}", [P, BANK], F32)) for n in range(8)]
        sbuf = Map(nc)
        ident = sbuf.put("own", "ident", [P, P])
        abs_sums = sbuf.put("own", "abs_sums", [P, 2, H])
        attention = attention_stage(nc, sem, sbuf, banks, ident, H, T, DM, DH, a["xT"], a["wq"], a["wk"], a["wv"],
                                    a["bqkv"], a["w1"], a["w2T"], abs_sums, z_dram, rinv_dram)
        sbuf.stage()
        w1_t = sbuf.put("v", "w1_t", [P, DM // P, F], F32R)
        w2_t = sbuf.put("v", "w2_t", [P, F // P, DM], F32R)
        projection = projection_stage(nc, sem, sbuf, banks, attention, H, T, DM, F, a["x"], a["wo"], a["bo"],
                                      a["w1T"], a["w2T"], abs_sums, w1_t, w2_t, z_dram, x1_dram)
        sbuf.stage()
        ffn = ffn_stage(nc, sem, sbuf, banks, ident, projection["b2_all"], projection, T, DM, F, w1_t, w2_t,
                        a["b1T"], a["b2"], x1_dram,
                        out)

        with nc.Block() as block:

            @block.sync
            def _(sp):
                attention["sync"](sp, projection["first_loads"], projection["second_loads"])
                projection["sync"](sp, lambda: ffn["load_first"](sp))
                ffn["sync"](sp)

            @block.gpsimd
            def _(pool):
                attention["gpsimd"](pool)
                projection["gpsimd"](pool)
                ffn["gpsimd"](pool)

            @block.scalar
            def _(act):
                attention["scalar"](act)
                projection["scalar"](act, lambda: ffn["transposed_hi"](act, 0))
                ffn["scalar"](act)

            @block.vector
            def _(dve):
                attention["vector"](dve)
                projection["vector"](dve, lambda: ffn["transposed_lo"](dve, 0))
                ffn["vector"](dve)

            @block.tensor
            def _(pe):
                attention["tensor"](pe, projection["first_heads"])
                projection["tensor"](pe, lambda: ffn["transpose_group"](pe, 0, 0))
                ffn["tensor"](pe)


def kernel(**inputs):
    import numpy as np
    import concourse.bacc as bacc
    from concourse.bass_utils import run_bass_kernel_spmd

    def get(name):
        return np.asarray(inputs["L0_" + name])

    x = get("attn_x")[0]
    w1, w2 = get("ffn_w1"), get("ffn_w2")
    F, DM = w1.shape
    arrays = {
        "x": x, "xT": x.T,
        "wq": get("attn_W_Q"), "wk": get("attn_W_K"), "wv": get("attn_W_V"), "wo": get("attn_W_O"),
        "bqkv": np.stack([get("attn_b_Q"), get("attn_b_K"), get("attn_b_V")], axis=-1), "bo": get("attn_b_O"),
        "w1": w1, "w1T": w1.T.reshape(DM // P, P, 2, F // 2).transpose(0, 2, 1, 3).reshape(-1, P, F // 2),
        "w2T": w2.T, "b1T": get("ffn_b1").reshape(F // P, P).T, "b2": get("ffn_b2"),
    }
    arrays = {n: np.ascontiguousarray(v) for n, v in arrays.items()}
    nc = bacc.Bacc("TRN2", target_bir_lowering=False, num_devices=1)
    aps = {n: nc.dram_tensor("in_" + n, v.shape, mybir.dt.from_np(v.dtype), kind="ExternalInput").ap()
           for n, v in arrays.items()}
    out = nc.dram_tensor("out", x.shape, F32, kind="ExternalOutput").ap()
    layer(nc, aps, out)
    r = run_bass_kernel_spmd(nc, [{"in_" + n: v for n, v in arrays.items()}], core_ids=[0])
    return r.results[0]["out"].reshape(1, *x.shape)
```
